# Optimizing a Trainium2 kernel written in Bass

```python
import numpy as np
import jax
import jax.numpy as jnp

def _softmax(x, axis=-1):
    return jax.nn.softmax(x, axis=axis)

def _gelu(x):
    return jax.nn.gelu(x, approximate=True)

def _silu(x):
    return jax.nn.silu(x)

def _sigmoid(x):
    return jax.nn.sigmoid(x)

def _layernorm(x, axis=-1, eps=1e-05):
    m = jnp.mean(x, axis=axis, keepdims=True)
    v = jnp.var(x, axis=axis, keepdims=True)
    return (x - m) / jnp.sqrt(v + eps)

def _scatter_add(tgt, idx, src, axis=0):
    return tgt.at[idx].add(src)

def _segment_sum(src, seg, n):
    return jax.ops.segment_sum(src, seg, n)
kernel_name = 'mk_gnn_ffn_d2_gnn_r32_1cc710'

def setup_inputs(seed: int=0):
    np.random.seed(seed)
    _w = jnp.asarray

    def _rec_inputs():
        import jax
        import jax.numpy as jnp
        _gk = jax.random.key(seed)
        x = -5.39e-05 + 0.9998 * jax.random.normal(jax.random.fold_in(_gk, 1), (3125, 256), jnp.float32)
        src = jax.random.randint(jax.random.fold_in(_gk, 2), (50000,), 0, 3125, jnp.int32)
        dst = jnp.minimum((3125 * jax.random.uniform(jax.random.fold_in(_gk, 3), (50000,)) ** 2.0).astype(jnp.int32), 99999)
        _o = jnp.argsort(dst, stable=True)
        src = src[_o]
        dst = dst[_o]
        edge_weight = jax.random.uniform(jax.random.fold_in(_gk, 13), (50000,), jnp.float32, 0.0, 1)
        return (x, src, dst, edge_weight)
    x, src, dst, edge_weight = _rec_inputs()

    def _L0_gnn_setup():
        import jax, jax.numpy as jnp
        import numpy as np
        N_NODES = 3125
        N_EDGES = 100000
        D_IN = 256
        D_OUT = 256
        key = jax.random.key(seed)
        k1, k2, k3, k4, k5 = jax.random.split(key, 5)
        bound = float(np.sqrt(6.0 / D_IN))
        weight = jax.random.uniform(k1, (D_IN, D_OUT), dtype=jnp.float32, minval=-bound, maxval=bound)
        bias = jnp.zeros((D_OUT,), dtype=jnp.float32)
        input_feature = jax.random.normal(k2, (N_NODES, D_IN), dtype=jnp.float32)
        edge_row = jax.random.randint(k3, (N_EDGES,), 0, N_NODES, dtype=jnp.int32)
        edge_col = jax.random.randint(k4, (N_EDGES,), 0, N_NODES, dtype=jnp.int32)
        edge_val = jax.random.uniform(k5, (N_EDGES,), dtype=jnp.float32)
        return {'input_feature': input_feature, 'weight': weight, 'bias': bias, 'edge_val': edge_val, 'edge_row': edge_row, 'edge_col': edge_col}
    _L0_gnn_all = _L0_gnn_setup()
    _L0_gnn_in = {k: v for k, v in _L0_gnn_all.items() if k in ('weight', 'bias')}
    del _L0_gnn_all

    def _L0_ffn_setup():
        import jax, jax.numpy as jnp
        import numpy as np
        B, N, D = (16, 128, 256)
        NUM_EXPERTS, TOP_K, HEADS = (4, 2, 4)
        N_EDGES = 32768
        LN_EPS = 1e-05

        def _layernorm(x, g, b):
            mu = x.mean(-1, keepdims=True)
            var = ((x - mu) ** 2).mean(-1, keepdims=True)
            return (x - mu) * jax.lax.rsqrt(var + LN_EPS) * g + b

        def _forward(x, edge_index, W_gat, att_src, att_dst, b_gat, ln_gamma, ln_beta, W1, b1, W2, b2):
            Bc, Nc, Dc = x.shape
            M = Bc * Nc
            x_flat = x.reshape(M, Dc)
            h = (x_flat @ W_gat).reshape(M, HEADS, NUM_EXPERTS)
            loops = jnp.arange(M, dtype=edge_index.dtype)
            src = jnp.concatenate([edge_index[0], loops])
            dst = jnp.concatenate([edge_index[1], loops])
            a_src = (h * att_src).sum(-1)
            a_dst = (h * att_dst).sum(-1)
            e = jax.nn.leaky_relu(a_src[src] + a_dst[dst], negative_slope=0.2)
            e_max = jax.ops.segment_max(e, dst, num_segments=M)
            ee = jnp.exp(e - e_max[dst])
            denom = jax.ops.segment_sum(ee, dst, num_segments=M)
            alpha = ee / (denom[dst] + 1e-16)
            msg = h[src] * alpha[:, :, None]
            agg = jax.ops.segment_sum(msg, dst, num_segments=M).reshape(M, HEADS * NUM_EXPERTS) + b_gat
            scores = _layernorm(agg, ln_gamma, ln_beta).reshape(M, HEADS, NUM_EXPERTS).mean(1)
            scores = scores.reshape(Bc, Nc, NUM_EXPERTS)
            topk_s, topk_i = jax.lax.top_k(scores, TOP_K)
            w = jax.nn.softmax(topk_s, axis=-1)
            out = jnp.zeros_like(x)
            for ei in range(NUM_EXPERTS):
                g = jnp.where(topk_i == ei, w, 0.0).sum(-1)
                hh = jax.nn.gelu(x @ W1[ei] + b1[ei], approximate=False)
                out = out + g[..., None] * (hh @ W2[ei] + b2[ei])
            return out
        key = jax.random.key(seed)
        ks = jax.random.split(key, 8)
        s = 0.05
        return {'x': jax.random.normal(ks[0], (B, N, D), jnp.float32), 'W_gat': jax.random.normal(ks[1], (D, HEADS * NUM_EXPERTS), jnp.float32) * s, 'att_src': jax.random.normal(ks[2], (HEADS, NUM_EXPERTS), jnp.float32) * s, 'att_dst': jax.random.normal(ks[3], (HEADS, NUM_EXPERTS), jnp.float32) * s, 'b_gat': jnp.zeros((HEADS * NUM_EXPERTS,), jnp.float32), 'ln_gamma': jnp.ones((HEADS * NUM_EXPERTS,), jnp.float32), 'ln_beta': jnp.zeros((HEADS * NUM_EXPERTS,), jnp.float32), 'W1': jax.random.normal(ks[4], (NUM_EXPERTS, D, 2 * D), jnp.float32) * s, 'b1': jnp.zeros((NUM_EXPERTS, 2 * D), jnp.float32), 'W2': jax.random.normal(ks[5], (NUM_EXPERTS, 2 * D, D), jnp.float32) * s, 'b2': jnp.zeros((NUM_EXPERTS, D), jnp.float32), 'edge_index': jax.random.randint(ks[6], (2, N_EDGES), 0, B * N, jnp.int32)}
    _L0_ffn_all = _L0_ffn_setup()
    _L0_ffn_in = {k: v for k, v in _L0_ffn_all.items() if k in ('W_gat', 'att_src', 'att_dst', 'b_gat', 'ln_gamma', 'ln_beta', 'W1', 'b1', 'W2', 'b2', 'edge_index')}
    del _L0_ffn_all

    def _L1_gnn_setup():
        import jax, jax.numpy as jnp
        import numpy as np
        N, E, H, C, IN = (50000, 15625, 4, 64, 256)

        def _gat_conv(x, src, dst, W, a_src, a_dst, b, n_nodes):
            Hh, Cc = a_src.shape
            h = (x @ W).reshape(n_nodes, Hh, Cc)
            e_src = jnp.einsum('nhc,hc->nh', h, a_src)
            e_dst = jnp.einsum('nhc,hc->nh', h, a_dst)
            e = jax.nn.leaky_relu(e_src[src] + e_dst[dst], 0.2)
            m = jax.lax.stop_gradient(jax.ops.segment_max(e, dst, num_segments=n_nodes))
            ex = jnp.exp(e - m[dst])
            denom = jax.ops.segment_sum(ex, dst, num_segments=n_nodes)
            alpha = ex / (denom[dst] + 1e-16)
            out = jax.ops.segment_sum(h[src] * alpha[:, :, None], dst, num_segments=n_nodes)
            return out.reshape(n_nodes, Hh * Cc) + b
        key = jax.random.key(seed)
        ks = jax.random.split(key, 16)
        sW = 1.0 / np.sqrt(IN)
        sA = 1.0 / np.sqrt(C)
        inp = {'x': jax.random.normal(ks[0], (N, IN), jnp.float32), 'edge_index': jax.random.randint(ks[1], (2, E), 0, N, jnp.int64 if jax.config.jax_enable_x64 else jnp.int32), 'W1': jax.random.normal(ks[2], (IN, H * C), jnp.float32) * sW, 'as1': jax.random.normal(ks[3], (H, C), jnp.float32) * sA, 'ad1': jax.random.normal(ks[4], (H, C), jnp.float32) * sA, 'b1': jnp.zeros((H * C,), jnp.float32), 'W2': jax.random.normal(ks[5], (H * C, H * C), jnp.float32) * sW, 'as2': jax.random.normal(ks[6], (H, C), jnp.float32) * sA, 'ad2': jax.random.normal(ks[7], (H, C), jnp.float32) * sA, 'b2': jnp.zeros((H * C,), jnp.float32), 'WN': jax.random.normal(ks[8], (H * C, H * C), jnp.float32) * sW, 'asN': jax.random.normal(ks[9], (H, C), jnp.float32) * sA, 'adN': jax.random.normal(ks[10], (H, C), jnp.float32) * sA, 'bN': jnp.zeros((H * C,), jnp.float32)}
        return inp
    _L1_gnn_all = _L1_gnn_setup()
    _L1_gnn_in = {k: v for k, v in _L1_gnn_all.items() if k in ('W1', 'as1', 'ad1', 'b1', 'W2', 'as2', 'ad2', 'b2', 'WN', 'asN', 'adN', 'bN')}
    del _L1_gnn_all

    def _L1_ffn_setup():
        import math
        import jax, jax.numpy as jnp
        import numpy as np
        CAPACITY_FACTOR = 1.25
        TOP_K = 2
        LN_EPS = 1e-05

        def _layer_norm(x, gamma, beta):
            mu = jnp.mean(x, axis=-1, keepdims=True)
            var = jnp.var(x, axis=-1, keepdims=True)
            return (x - mu) * jax.lax.rsqrt(var + LN_EPS) * gamma + beta
        key = jax.random.key(seed)
        ks = jax.random.split(key, 4)
        B, S, D, F, E = (8, 128, 256, 512, 8)
        x = jax.random.normal(ks[0], (B, S, D), dtype=jnp.float32)
        Wr = jax.random.normal(ks[1], (D, E), dtype=jnp.float32) / np.sqrt(D)
        br = jnp.zeros((E,), jnp.float32)
        W1 = jax.random.normal(ks[2], (E, D, F), dtype=jnp.float32) / np.sqrt(D)
        b1 = jnp.zeros((E, F), jnp.float32)
        W2 = jax.random.normal(ks[3], (E, F, D), dtype=jnp.float32) / np.sqrt(F)
        b2 = jnp.zeros((E, D), jnp.float32)
        gamma = jnp.ones((D,), jnp.float32)
        beta = jnp.zeros((D,), jnp.float32)
        return {'x': x, 'Wr': Wr, 'br': br, 'W1': W1, 'b1': b1, 'W2': W2, 'b2': b2, 'gamma': gamma, 'beta': beta}
    _L1_ffn_all = _L1_ffn_setup()
    _L1_ffn_in = {k: v for k, v in _L1_ffn_all.items() if k in ('Wr', 'br', 'W1', 'b1', 'W2', 'b2', 'gamma', 'beta')}
    del _L1_ffn_all
    return {'x': x, 'src': src, 'dst': dst, 'edge_weight': edge_weight, 'L0_gnn_weight': _L0_gnn_in['weight'], 'L0_gnn_bias': _L0_gnn_in['bias'], 'L0_ffn_W_gat': _L0_ffn_in['W_gat'], 'L0_ffn_att_src': _L0_ffn_in['att_src'], 'L0_ffn_att_dst': _L0_ffn_in['att_dst'], 'L0_ffn_b_gat': _L0_ffn_in['b_gat'], 'L0_ffn_ln_gamma': _L0_ffn_in['ln_gamma'], 'L0_ffn_ln_beta': _L0_ffn_in['ln_beta'], 'L0_ffn_W1': _L0_ffn_in['W1'], 'L0_ffn_b1': _L0_ffn_in['b1'], 'L0_ffn_W2': _L0_ffn_in['W2'], 'L0_ffn_b2': _L0_ffn_in['b2'], 'L0_ffn_edge_index': _L0_ffn_in['edge_index'], 'L1_gnn_W1': _L1_gnn_in['W1'], 'L1_gnn_as1': _L1_gnn_in['as1'], 'L1_gnn_ad1': _L1_gnn_in['ad1'], 'L1_gnn_b1': _L1_gnn_in['b1'], 'L1_gnn_W2': _L1_gnn_in['W2'], 'L1_gnn_as2': _L1_gnn_in['as2'], 'L1_gnn_ad2': _L1_gnn_in['ad2'], 'L1_gnn_b2': _L1_gnn_in['b2'], 'L1_gnn_WN': _L1_gnn_in['WN'], 'L1_gnn_asN': _L1_gnn_in['asN'], 'L1_gnn_adN': _L1_gnn_in['adN'], 'L1_gnn_bN': _L1_gnn_in['bN'], 'L1_ffn_Wr': _L1_ffn_in['Wr'], 'L1_ffn_br': _L1_ffn_in['br'], 'L1_ffn_W1': _L1_ffn_in['W1'], 'L1_ffn_b1': _L1_ffn_in['b1'], 'L1_ffn_W2': _L1_ffn_in['W2'], 'L1_ffn_b2': _L1_ffn_in['b2'], 'L1_ffn_gamma': _L1_ffn_in['gamma'], 'L1_ffn_beta': _L1_ffn_in['beta']}

def reference(x, src, dst, edge_weight, L0_gnn_weight, L0_gnn_bias, L0_ffn_W_gat, L0_ffn_att_src, L0_ffn_att_dst, L0_ffn_b_gat, L0_ffn_ln_gamma, L0_ffn_ln_beta, L0_ffn_W1, L0_ffn_b1, L0_ffn_W2, L0_ffn_b2, L0_ffn_edge_index, L1_gnn_W1, L1_gnn_as1, L1_gnn_ad1, L1_gnn_b1, L1_gnn_W2, L1_gnn_as2, L1_gnn_ad2, L1_gnn_b2, L1_gnn_WN, L1_gnn_asN, L1_gnn_adN, L1_gnn_bN, L1_ffn_Wr, L1_ffn_br, L1_ffn_W1, L1_ffn_b1, L1_ffn_W2, L1_ffn_b2, L1_ffn_gamma, L1_ffn_beta):
    import jax
    import jax.numpy as jnp

    def _L0_gnn_ref(input_feature, weight, bias, edge_val, edge_row, edge_col):
        import jax, jax.numpy as jnp
        import numpy as np
        N_NODES = 3125
        N_EDGES = 100000
        D_IN = 256
        D_OUT = 256
        support = input_feature @ weight
        messages = edge_val[:, None] * support[edge_col]
        output = jax.ops.segment_sum(messages, edge_row, num_segments=N_NODES)
        return output + bias

    def _L0_ffn_ref(x, W_gat, att_src, att_dst, b_gat, ln_gamma, ln_beta, W1, b1, W2, b2, edge_index):
        import jax, jax.numpy as jnp
        import numpy as np
        B, N, D = (16, 128, 256)
        NUM_EXPERTS, TOP_K, HEADS = (4, 2, 4)
        N_EDGES = 32768
        LN_EPS = 1e-05

        def _layernorm(x, g, b):
            mu = x.mean(-1, keepdims=True)
            var = ((x - mu) ** 2).mean(-1, keepdims=True)
            return (x - mu) * jax.lax.rsqrt(var + LN_EPS) * g + b

        def _forward(x, edge_index, W_gat, att_src, att_dst, b_gat, ln_gamma, ln_beta, W1, b1, W2, b2):
            Bc, Nc, Dc = x.shape
            M = Bc * Nc
            x_flat = x.reshape(M, Dc)
            h = (x_flat @ W_gat).reshape(M, HEADS, NUM_EXPERTS)
            loops = jnp.arange(M, dtype=edge_index.dtype)
            src = jnp.concatenate([edge_index[0], loops])
            dst = jnp.concatenate([edge_index[1], loops])
            a_src = (h * att_src).sum(-1)
            a_dst = (h * att_dst).sum(-1)
            e = jax.nn.leaky_relu(a_src[src] + a_dst[dst], negative_slope=0.2)
            e_max = jax.ops.segment_max(e, dst, num_segments=M)
            ee = jnp.exp(e - e_max[dst])
            denom = jax.ops.segment_sum(ee, dst, num_segments=M)
            alpha = ee / (denom[dst] + 1e-16)
            msg = h[src] * alpha[:, :, None]
            agg = jax.ops.segment_sum(msg, dst, num_segments=M).reshape(M, HEADS * NUM_EXPERTS) + b_gat
            scores = _layernorm(agg, ln_gamma, ln_beta).reshape(M, HEADS, NUM_EXPERTS).mean(1)
            scores = scores.reshape(Bc, Nc, NUM_EXPERTS)
            topk_s, topk_i = jax.lax.top_k(scores, TOP_K)
            w = jax.nn.softmax(topk_s, axis=-1)
            out = jnp.zeros_like(x)
            for ei in range(NUM_EXPERTS):
                g = jnp.where(topk_i == ei, w, 0.0).sum(-1)
                hh = jax.nn.gelu(x @ W1[ei] + b1[ei], approximate=False)
                out = out + g[..., None] * (hh @ W2[ei] + b2[ei])
            return out
        return _forward(x, edge_index, W_gat, att_src, att_dst, b_gat, ln_gamma, ln_beta, W1, b1, W2, b2)

    def _L1_gnn_ref(x, edge_index, W1, as1, ad1, b1, W2, as2, ad2, b2, WN, asN, adN, bN):
        import jax, jax.numpy as jnp
        import numpy as np
        N, E, H, C, IN = (50000, 15625, 4, 64, 256)

        def _gat_conv(x, src, dst, W, a_src, a_dst, b, n_nodes):
            Hh, Cc = a_src.shape
            h = (x @ W).reshape(n_nodes, Hh, Cc)
            e_src = jnp.einsum('nhc,hc->nh', h, a_src)
            e_dst = jnp.einsum('nhc,hc->nh', h, a_dst)
            e = jax.nn.leaky_relu(e_src[src] + e_dst[dst], 0.2)
            m = jax.lax.stop_gradient(jax.ops.segment_max(e, dst, num_segments=n_nodes))
            ex = jnp.exp(e - m[dst])
            denom = jax.ops.segment_sum(ex, dst, num_segments=n_nodes)
            alpha = ex / (denom[dst] + 1e-16)
            out = jax.ops.segment_sum(h[src] * alpha[:, :, None], dst, num_segments=n_nodes)
            return out.reshape(n_nodes, Hh * Cc) + b
        n = x.shape[0]
        loops = jnp.arange(n, dtype=edge_index.dtype)
        src = jnp.concatenate([edge_index[0], loops])
        dst = jnp.concatenate([edge_index[1], loops])
        inp = x
        h = jax.nn.relu(_gat_conv(x, src, dst, W1, as1, ad1, b1, n)) + inp
        h = jax.nn.relu(_gat_conv(h, src, dst, W2, as2, ad2, b2, n))
        h = _gat_conv(h, src, dst, WN, asN, adN, bN, n)
        return jax.nn.relu(h + inp)

    def _L1_ffn_ref(x, Wr, br, W1, b1, W2, b2, gamma, beta):
        import math
        import jax, jax.numpy as jnp
        import numpy as np
        CAPACITY_FACTOR = 1.25
        TOP_K = 2
        LN_EPS = 1e-05

        def _layer_norm(x, gamma, beta):
            mu = jnp.mean(x, axis=-1, keepdims=True)
            var = jnp.var(x, axis=-1, keepdims=True)
            return (x - mu) * jax.lax.rsqrt(var + LN_EPS) * gamma + beta
        B, S, D = x.shape
        E = Wr.shape[1]
        N = B * S
        K = TOP_K
        logits = jnp.mean(x, axis=1) @ Wr + br
        routing_weights = jax.nn.softmax(logits, axis=-1)
        capacity = float(math.ceil(N * CAPACITY_FACTOR / E))
        expected_loads = routing_weights.sum(axis=0) * (N / B)
        scale = jnp.where(expected_loads > capacity, capacity / expected_loads, 1.0)
        routing_weights = jax.nn.softmax(routing_weights * scale, axis=-1)
        rw_tok = jnp.broadcast_to(routing_weights[:, None, :], (B, S, E)).reshape(N, E)
        top_w, top_i = jax.lax.top_k(rw_tok, K)
        top_w = jax.nn.softmax(top_w, axis=-1)
        xf = x.reshape(N, D)
        h = jax.nn.gelu(jnp.einsum('nd,edf->enf', xf, W1) + b1[:, None, :], approximate=False)
        y = jnp.einsum('enf,efd->end', h, W2) + b2[:, None, :]
        w_dense = jnp.zeros((N, E), x.dtype).at[jnp.arange(N)[:, None], top_i].add(top_w)
        out = jnp.einsum('ne,end->nd', w_dense, y).reshape(B, S, D)
        out = _layer_norm(out + x, gamma, beta)
        return out
    edge_index = jnp.stack([src, dst])
    x = x + _L0_gnn_ref(_layernorm(x, axis=-1), L0_gnn_weight, L0_gnn_bias, edge_weight, src, dst)
    x = x + _L0_ffn_ref(_layernorm(x, axis=-1)[None], L0_ffn_W_gat, L0_ffn_att_src, L0_ffn_att_dst, L0_ffn_b_gat, L0_ffn_ln_gamma, L0_ffn_ln_beta, L0_ffn_W1, L0_ffn_b1, L0_ffn_W2, L0_ffn_b2, L0_ffn_edge_index)[0]
    x = x + _L1_gnn_ref(_layernorm(x, axis=-1), edge_index, L1_gnn_W1, L1_gnn_as1, L1_gnn_ad1, L1_gnn_b1, L1_gnn_W2, L1_gnn_as2, L1_gnn_ad2, L1_gnn_b2, L1_gnn_WN, L1_gnn_asN, L1_gnn_adN, L1_gnn_bN)
    x = x + _L1_ffn_ref(_layernorm(x, axis=-1)[None], L1_ffn_Wr, L1_ffn_br, L1_ffn_W1, L1_ffn_b1, L1_ffn_W2, L1_ffn_b2, L1_ffn_gamma, L1_ffn_beta)[0]
    return x

_drawn_inputs = setup_inputs


def setup_inputs(seed=0):
    import zlib

    import numpy as np

    out = dict(_drawn_inputs(seed))
    spreads = {'L0_gnn_bias': (0.0, 0.1),
     'L0_ffn_b_gat': (0.0, 0.1),
     'L0_ffn_ln_gamma': (1.0, 0.2),
     'L0_ffn_ln_beta': (0.0, 0.375),
     'L0_ffn_b1': (0.0, 0.495),
     'L0_ffn_b2': (0.0, 0.37),
     'L1_gnn_b1': (0.0, 0.8),
     'L1_gnn_b2': (0.0, 0.732),
     'L1_gnn_bN': (0.0, 0.46),
     'L1_ffn_br': (0.0, 0.1),
     'L1_ffn_b1': (0.0, 0.8),
     'L1_ffn_b2': (0.0, 0.584),
     'L1_ffn_gamma': (1.0, 0.2),
     'L1_ffn_beta': (0.0, 0.411)}
    factors = {'L0_ffn_att_src': 4.788,
     'L0_ffn_att_dst': 6.952,
     'L1_gnn_W1': 7.393,
     'L1_gnn_as1': 8.0,
     'L1_gnn_ad1': 8.0,
     'L1_gnn_as2': 4.537,
     'L1_gnn_ad2': 8.0,
     'L1_gnn_asN': 8.0,
     'L1_gnn_adN': 8.0}
    for name, (base, spread) in spreads.items():
        noise = np.random.default_rng([zlib.crc32(name.encode()), seed]).standard_normal(out[name].shape)
        drawn = base * np.exp(spread * noise) if base else spread * noise
        out[name] = jnp.asarray(drawn.astype(out[name].dtype))
    for name, factor in factors.items():
        out[name] = (out[name] * factor).astype(out[name].dtype)
    return out
```

```python
from contextlib import ExitStack

import concourse.bass as bass
from concourse import mybir

P = 128
N = 3125
D = 256
E = 50000
EG = 32768
NT = (N + P - 1) // P
LAST = N - (NT - 1) * P
ET = 4
CH = ET * P
F = 512
COPIES = 8
GN = 5
HEADS = 4
LN_EPS = 1e-5
BIG = 1e30

ALU = mybir.AluOpType
ACT = mybir.ActivationFunctionType
AX = mybir.AxisListType
F32 = mybir.dt.float32
BF16 = mybir.dt.bfloat16
I32 = mybir.dt.int32


def chunks_for(edges):
    worst = (edges + NT * (CH - 1)) // CH
    return -(-worst // 6) * 6


NCH = chunks_for(E)
NCHG = chunks_for(EG)


class Chain:

    def __init__(self, eng, sem):
        self.eng, self.sem, self.n, self.base, self.i, self.per = eng, sem, 0, 0, None, 0

    def enter(self, i, per):
        self.i, self.per, self.base, self.n = i, per, self.base + self.n, 0

    def leave(self, trips):
        assert self.n == self.per, (self.n, self.per)
        self.i, self.base, self.n = None, self.base + self.per * trips, 0

    def next(self, ins):
        ins.then_inc(self.sem, 1)
        self.n += 1
        at = self.base + self.n
        self.eng.wait_ge(self.sem, at if self.i is None else self.i * self.per + at)



def setup(nc, block, m, x_in):
    made, loaded, zeroed, iotas = m.sem("const_made"), m.sem("x_loaded"), m.sem("x_zeroed"), m.sem("iota_made")
    steps = m.sem("setup_steps")

    @block.gpsimd
    def _(pool):
        nc.gpsimd.memset(m.ident[:, :], 0.0).then_inc(made, 1)
        nc.gpsimd.memset(m.before[:, :], 1.0).then_inc(made, 1)
        nc.gpsimd.iota(m.iota_i[:, :], pattern=[[1, P]], base=0, channel_multiplier=0).then_inc(iotas, 1)
        nc.gpsimd.iota(m.iota_c[:, :], pattern=[[1, NCH]], base=0, channel_multiplier=0).then_inc(iotas, 1)
        nc.gpsimd.iota(m.pid_i[:, :], pattern=[[1, 2]], base=0, channel_multiplier=1).then_inc(iotas, 1)
        pool.wait_ge(made, 2)
        nc.gpsimd.affine_select(out=m.ident[:, :], in_=m.ident[:, :], compare_op=ALU.not_equal, fill=1.0, base=0,
                                pattern=[[-1, P]], channel_multiplier=1).then_inc(made, 1)
        nc.gpsimd.affine_select(out=m.before[:, :], in_=m.before[:, :], compare_op=ALU.is_gt, fill=0.0, base=0,
                                pattern=[[1, P]], channel_multiplier=-1).then_inc(made, 1)
        pool.wait_ge(made, 4)

    @block.vector
    def _(dve):
        nc.vector.memset(m.x[:, NT - 1, :], 0.0).then_inc(zeroed, 1)
        nc.vector.memset(m.ones[:, :], 1.0)
        dve.wait_ge(iotas, 3)
        nc.vector.tensor_copy(m.iota[:, :], m.iota_i[:, :])
        nc.vector.tensor_copy(m.iotac[:, :], m.iota_c[:, :])
        nc.vector.tensor_copy(m.pid[:, :], m.pid_i[:, :]).then_inc(steps, 1)
        dve.wait_ge(steps, 1)
        nc.vector.tensor_scalar(m.dummy[:, 0:1], m.pid[:, 0:1], float(P * ET * NCH), None, ALU.add)
        nc.vector.tensor_scalar(m.dummy[:, 1:2], m.pid[:, 0:1], float(P * ET * NCHG), None, ALU.add)
        nc.vector.tensor_tensor(m.lower[:, :, :], m.iota[:, 0:8].unsqueeze(1).to_broadcast([P, 8, 8]),
                                m.iota[:, 0:8].unsqueeze(2).to_broadcast([P, 8, 8]), ALU.is_lt).then_inc(steps, 1)
        dve.wait_ge(steps, 2)

    @block.sync
    def _(sp):
        sp.dma_start(m.x[:, 0:NT - 1, :], x_in[0:(NT - 1) * P, :].rearrange("(t p) d -> p t d", p=P)).then_inc(loaded, 16)
        sp.wait_ge(zeroed, 1)
        sp.dma_start(m.x[0:LAST, NT - 1, :], x_in[(NT - 1) * P:N, :]).then_inc(loaded, 16)
        sp.wait_ge(loaded, 32)



def sort_edges(nc, block, m, name, key_in, val_in, w_in, nch, rec_dram, rec, bucket):
    edges = key_in.shape[0]
    fc = 400 if edges == E else 256
    pf = edges // fc
    assert pf * fc == edges and fc % COPIES == 0
    ncol = nch * ET
    dummy = P * ncol
    half = COPIES // 2
    trips = fc // COPIES

    loaded, cleared, rec_filled, passed = (m.sem(f"{name}_{s}") for s in ("loaded", "cleared", "recfilled", "passed"))
    steps, ends, sums, placed, staged, back = (m.sem(f"{name}_{s}") for s in ("steps", "ends", "sums", "placed", "staged", "back"))
    sent = [m.dma_sem(f"{name}_sent{s}") for s in range(2)]
    key, hi, val = m.sort_key[:, 0:fc], m.sort_hi[:, 0:fc], m.sort_val[:, 0:fc]
    w, lo_f, val_f = m.sort_w[:, 0:fc], m.sort_lo_f[:, 0:fc], m.sort_val_f[:, 0:fc]
    lo_i, place, row = m.sort_lo[:, 0:fc], m.sort_place[:, 0:fc], m.sort_row[:, 0:fc]
    mask = m.work[:, 10000:15000].bitcast(BF16)[:, 0:NT * fc].rearrange("p (b f) -> p b f", b=NT)
    count = m.work[:, 0:NT * fc].rearrange("p (b f) -> p b f", b=NT)
    small = m.sort_small
    cum, prev, own = small[:, 0, 0:NT], small[:, 1, :], small[:, 2, 0:NT]
    total, nchunk, cend, add = small[:, 3, 0:NT], small[:, 4, 0:NT], small[:, 5, 0:NT], small[:, 6, 0:NT]
    total_i = m.sort_small_i[:, :]
    ps_before, ps_total = m.psum[0][:, 0:NT], m.psum[0][:, 64:64 + NT]
    parts = m.work[:, 0:COPIES * 3 * ncol].rearrange("p (k c) -> p k c", k=COPIES)

    @block.sync
    def _(sp):
        sp.wait_ge(cleared, 1)
        sp.dma_start(key[0:pf, :], key_in.rearrange("(p f) -> p f", f=fc)).then_inc(loaded, 16)
        sp.dma_start(val[0:pf, :], val_in.rearrange("(p f) -> p f", f=fc)).then_inc(loaded, 16)
        if w_in is not None:
            sp.dma_start(w[0:pf, :], w_in.rearrange("(p f) -> p f", f=fc)).then_inc(loaded, 16)
        for k in range(COPIES):
            sp.dma_start(rec_dram[k][0:dummy, :].rearrange("(p c) k -> p (c k)", p=P), m.work[:, 0:3 * ncol]).then_inc(rec_filled, 16)
        for s in range(2):
            sp.wait_ge(sent[s], trips * half * 16)
        for k in range(COPIES):
            sp.dma_start(parts[:, k, :], rec_dram[k][0:dummy, :].rearrange("(p c) k -> p (c k)", p=P)).then_inc(back, 16)

    @block.tensor
    def _(pe):
        pe.wait_ge(ends, 1)
        nc.tensor.matmul(ps_before, m.before[:, :], own, start=True, stop=True)
        nc.tensor.matmul(ps_total, m.ones[:, :], own, start=True, stop=True).then_inc(sums, 1)

    @block.vector
    def _(dve):
        chain = Chain(dve, steps)
        nc.vector.memset(key, NT * P)
        nc.vector.memset(val, 0)
        nc.vector.memset(w, 0.0)
        nc.vector.memset(prev, 0.0)
        nc.vector.memset(m.work[:, 0:3 * ncol], 0.0).then_inc(cleared, 1)
        dve.wait_ge(cleared, 1)
        dve.wait_ge(loaded, 48 if w_in is not None else 32)
        nc.vector.tensor_scalar(lo_i, key, P - 1, None, ALU.bitwise_and)
        chain.next(nc.vector.tensor_scalar(place, key, 7, None, ALU.logical_shift_right))
        chain.next(nc.vector.tensor_copy(hi, place))
        chain.next(nc.vector.tensor_tensor(mask, hi.unsqueeze(1).to_broadcast([P, NT, fc]),
                                           m.iota[:, 0:NT].unsqueeze(2).to_broadcast([P, NT, fc]), ALU.is_equal))
        dve.wait_ge(rec_filled, 16 * COPIES)
        flat = m.work[:, 10000:15000].bitcast(BF16)[:, 0:NT * fc]
        chain.next(nc.vector.tensor_tensor_scan(m.work[:, 0:NT * fc], m.ones[:, 0:1].to_broadcast([P, NT * fc]), flat,
                                                0.0, ALU.mult, ALU.add))
        chain.next(nc.vector.tensor_copy(cum, count[:, :, fc - 1]))
        nc.vector.tensor_copy(prev[:, 1:NT], cum[:, 0:NT - 1]).then_inc(placed, 1)
        dve.wait_ge(placed, 1)
        nc.vector.tensor_tensor(own, cum, prev[:, 0:NT], ALU.subtract).then_inc(ends, 1)
        dve.wait_ge(sums, 1)
        chain.next(nc.vector.tensor_scalar(total, ps_total, float(CH - 1), None, ALU.add))
        chain.next(nc.vector.tensor_copy(total_i, total))
        chain.next(nc.vector.tensor_scalar(total_i, total_i, 9, None, ALU.logical_shift_right))
        chain.next(nc.vector.tensor_copy(nchunk, total_i))
        chain.next(nc.vector.tensor_tensor_scan(cend, m.ones[:, 0:NT], nchunk, 0.0, ALU.mult, ALU.add))
        chain.next(nc.vector.tensor_tensor(add, cend, nchunk, ALU.subtract))
        chain.next(nc.vector.scalar_tensor_tensor(add, add, float(CH), ps_before, ALU.mult, ALU.add))
        chain.next(nc.vector.tensor_tensor(add, add, prev[:, 0:NT], ALU.subtract))
        chain.next(nc.vector.tensor_scalar(add, add, -1.0, None, ALU.add))
        chain.next(nc.vector.tensor_tensor(count, count, add.unsqueeze(2).to_broadcast([P, NT, fc]), ALU.add))
        chain.next(nc.vector.tensor_tensor(count, count, mask, ALU.mult))
        chain.next(nc.vector.tensor_reduce(hi, count.rearrange("p b f -> p f b"), AX.X, ALU.add))
        chain.next(nc.vector.tensor_copy(place, hi))
        nc.vector.tensor_scalar(m.sort_hi2[:, 0:fc], key, float(NT * P), m.dummy[:, 0:1] if nch == NCH else m.dummy[:, 1:2], ALU.is_ge, ALU.mult)
        chain.next(nc.vector.tensor_scalar(row, place, P - 1, None, ALU.bitwise_and))
        chain.next(nc.vector.tensor_scalar(place, place, 7, None, ALU.logical_shift_right))
        chain.next(nc.vector.scalar_tensor_tensor(hi, row, float(ncol), place, ALU.mult, ALU.add))
        chain.next(nc.vector.tensor_tensor(row, hi, m.sort_hi2[:, 0:fc], ALU.add))
        cmp = m.work[:, 0:NT * nch].rearrange("p (c b) -> p c b", b=NT)
        chain.next(nc.vector.tensor_tensor(cmp, cend.unsqueeze(1).to_broadcast([P, nch, NT]),
                                           m.iotac[:, 0:nch].unsqueeze(2).to_broadcast([P, nch, NT]), ALU.is_le))
        chain.next(nc.vector.tensor_reduce(m.sort_hi2[:, 0:nch], cmp, AX.X, ALU.add))
        chain.next(nc.vector.tensor_copy(bucket[:, 0:nch], m.sort_hi2[:, 0:nch]))
        chain.next(nc.vector.tensor_scalar(lo_f, lo_i, 1.0, None, ALU.add))
        chain.next(nc.vector.tensor_copy(val_f, val))
        def stage(at, s):
            for q, column in enumerate((lo_f, val_f, w)):
                nc.vector.tensor_scalar(m.stage_rec[s][:, :, q], column[:, bass.ds(at, half)], 0.0, None, ALU.add)
            nc.vector.tensor_scalar(m.stage_row[s][:, :], row[:, bass.ds(at, half)], 0.0, None, ALU.add).then_inc(staged, 1)

        for s in range(2):
            stage(half * s, s)
        with dve.Fori(1, trips) as i:
            for s in range(2):
                dve.wait_ge(sent[s], i * (half * 16))
                stage(i * COPIES + half * s, s)
        dve.wait_ge(back, 16 * COPIES)
        for k in range(0, COPIES, 2):
            nc.vector.tensor_tensor(parts[:, k, :], parts[:, k, :], parts[:, k + 1, :], ALU.add)
        chain.next(nc.vector.tensor_copy(m.small[:, 0:1], m.ones[:, 0:1]))
        for k in range(0, COPIES, 4):
            chain.next(nc.vector.tensor_tensor(parts[:, k, :], parts[:, k, :], parts[:, k + 2, :], ALU.add))
        chain.next(nc.vector.tensor_tensor(rec, parts[:, 0, :], parts[:, 4, :], ALU.add))
        low = rec.rearrange("p (c k) -> p c k", k=3)[:, :, 0]
        chain.next(nc.vector.tensor_scalar(low, low, -1.0, None, ALU.add))

    @block.gpsimd
    def _(pool):
        pool.wait_ge(rec_filled, 16 * COPIES)
        with pool.Fori(0, trips) as i:
            for s in range(2):
                pool.wait_ge(staged, i * 2 + s + 1)
                pool.sem_inc(passed, 1)
                for f in range(half):
                    nc.gpsimd.indirect_dma_start(
                        out=rec_dram[s * half + f], out_offset=bass.IndirectOffsetOnAxis(ap=m.stage_row[s][:, f:f + 1], axis=0),
                        in_=m.stage_rec[s][:, f, :], in_offset=None).then_inc(sent[s], 16)



def norm_rows(nc, block, m, name, src, dst, tiles=NT):
    steps, var_ready, std_ready = m.sem(f"{name}_steps"), m.sem(f"{name}_var"), m.sem(f"{name}_std")
    square = m.work[:, 0:tiles * D].rearrange("p (t d) -> p t d", t=tiles)
    mean, var, std = (m.stats[:, k, 0:tiles] for k in range(3))

    def wide(a):
        return a.unsqueeze(2).to_broadcast([P, tiles, D])

    @block.vector
    def _(dve):
        chain = Chain(dve, steps)
        chain.next(nc.vector.tensor_reduce(mean, src, AX.X, ALU.add))
        chain.next(nc.vector.tensor_scalar(mean, mean, 1.0 / D, None, ALU.mult))
        chain.next(nc.vector.tensor_tensor(dst, src, wide(mean), ALU.subtract))
        chain.next(nc.vector.tensor_tensor(square, dst, dst, ALU.mult))
        chain.next(nc.vector.tensor_reduce(var, square, AX.X, ALU.add))
        nc.vector.tensor_scalar(var, var, 1.0 / D, LN_EPS, ALU.mult, ALU.add).then_inc(var_ready, 1)
        dve.wait_ge(std_ready, 1)
        chain.next(nc.vector.reciprocal(std, std))
        chain.next(nc.vector.tensor_tensor(dst, dst, wide(std), ALU.mult))

    @block.scalar
    def _(act):
        act.wait_ge(var_ready, 1)
        nc.scalar.activation(std, var, ACT.Sqrt).then_inc(std_ready, 1)



def project(nc, block, m, name, w_in, width, src, table, att_src=None, att_dst=None, keep_t=None):
    dh = width // HEADS
    rw = width + 2 * HEADS if att_src is not None else width
    staged, turned, turned_sb, done, taken, rows, stored, w_loaded, mult = (
        m.sem(f"{name}_{s}") for s in ("staged", "turned", "turnedsb", "done", "taken", "rows", "stored", "wloaded", "mult"))
    xs, xt = m.slot_x, m.slot_xt
    TB = 3
    ps_t = [m.psum[j % TB][:, 0:2 * P].rearrange("p (k n) -> p k n", k=2) for j in range(GN)]
    ps_h = [m.psum[TB + j][:, 0:width] for j in range(GN)]
    wt = m.w_mat[:, :, 0:width]
    acc = m.acc
    trips = NT // GN

    @block.sync
    def _(sp):
        sp.dma_start(wt, w_in.rearrange("(k p) n -> p k n", p=P)).then_inc(w_loaded, 16)
        if att_src is not None:
            sp.dma_start(m.att[:, 0, 0:width], att_src.rearrange("h c -> (h c)").partition_broadcast(P)).then_inc(w_loaded, 16)
            sp.dma_start(m.att[:, 1, 0:width], att_dst.rearrange("h c -> (h c)").partition_broadcast(P)).then_inc(w_loaded, 16)
        with sp.Fori(0, trips) as i:
            for j in range(GN):
                sp.wait_ge(taken if att_src is None else rows, i * GN + j + (2 if att_src is None else 1))
                sp.dma_start(table[bass.ds(i * (GN * P) + j * P, P), 0:rw], acc[:, i * GN + j, 0:rw]).then_inc(stored, 16)
        sp.wait_ge(stored, 16 * NT)

    @block.scalar
    def _(act):
        act.sem_inc(turned_sb, 1)
        with act.Fori(0, trips) as i:
            for j in range(GN):
                act.wait_ge(turned, i * GN + 1)
                nc.scalar.copy(xs[j][:, :], src[:, i * GN + j, :]).then_inc(staged, 1)
            for j in range(GN):
                act.wait_ge(turned, i * GN + j + 2)
                act.wait_ge(done, i * GN + 1)
                nc.scalar.copy(xt[j][:, :, :], ps_t[j]).then_inc(turned_sb, 1)
                if keep_t is not None:
                    nc.scalar.copy(keep_t[:, :, bass.ds(i * (GN * P) + j * P, P)], ps_t[j]).then_inc(turned_sb, 1)

    per = 2 if keep_t is not None else 1

    @block.tensor
    def _(pe):
        pe.sem_inc(turned, 1)
        pe.sem_inc(done, 1)
        with pe.Fori(0, trips) as i:
            for j in range(GN):
                pe.wait_ge(staged, i * GN + j + 1)
                pe.wait_ge(turned_sb, i * (GN * per) + (max(0, j - TB + 1) * per + 1))
                for k in range(2):
                    ins = nc.tensor.transpose(ps_t[j][:, k, :], xs[j][:, k * P:(k + 1) * P], m.ident[:, :])
                ins.then_inc(turned, 1)
            for j in range(GN):
                pe.wait_ge(turned_sb, i * (GN * per) + ((j + 1) * per + 1))
                pe.wait_ge(w_loaded, 16 if att_src is None else 48)
                pe.wait_ge(taken, i * GN + 1)
                for k in range(2):
                    ins = nc.tensor.matmul(ps_h[j], xt[j][:, k, :], wt[:, k, :], start=k == 0, stop=k == 1)
                ins.then_inc(done, 1)

    @block.vector
    def _(dve):
        chain = Chain(dve, mult)
        dve.sem_inc(taken, 1)
        if att_src is not None:
            dve.wait_ge(w_loaded, 48)
        with dve.Fori(0, trips) as i:
            chain.enter(i, 0 if att_src is None else 2 * GN)
            for j in range(GN):
                t = i * GN + j
                dve.wait_ge(done, i * GN + j + 2)
                if att_src is None:
                    nc.vector.tensor_scalar(acc[:, t, 0:width], ps_h[j], 0.0, None, ALU.add).then_inc(taken, 1)
                    continue
                heads = acc[:, t, 0:width + HEADS].rearrange("p (h w) -> p h w", h=HEADS)
                prod, sm = m.prod, m.small
                nc.vector.tensor_scalar(heads[:, :, 0:dh], ps_h[j].rearrange("p (h c) -> p h c", h=HEADS), 0.0, None, ALU.add)
                nc.vector.tensor_scalar(heads[:, :, dh], m.ones[:, 0:HEADS], 1.0, None, ALU.mult)
                nc.vector.tensor_tensor(prod[:, 1, 0:width], ps_h[j], m.att[:, 1, 0:width], ALU.mult)
                nc.vector.tensor_tensor(prod[:, 0, 0:width], ps_h[j], m.att[:, 0, 0:width], ALU.mult).then_inc(taken, 1)
                dve.wait_ge(taken, t + 2)
                nc.vector.tensor_reduce(m.state[:, t, 0:HEADS], prod[:, 1, 0:width].rearrange("p (h c) -> p h c", h=HEADS), AX.X, ALU.add)
                nc.vector.tensor_reduce(acc[:, t, width + HEADS:rw], prod[:, 0, 0:width].rearrange("p (h c) -> p h c", h=HEADS),
                                        AX.X, ALU.add).then_inc(rows, 1)
                dve.wait_ge(rows, t + 1)
                chain.next(nc.vector.tensor_tensor(sm[:, 0:HEADS], m.state[:, t, 0:HEADS], acc[:, t, width + HEADS:rw], ALU.add))
                chain.next(nc.vector.scalar_tensor_tensor(m.state[:, t, HEADS:2 * HEADS], sm[:, 0:HEADS], 0.2, sm[:, 0:HEADS],
                                                          ALU.mult, ALU.max))
        chain.leave(trips)



def sum_edges(nc, block, m, name, table, rec, bucket, nch):
    passed, copied, staged, hot, summed, taken, out = (m.sem(f"{name}_{s}") for s in ("passed", "copied", "staged", "hot", "summed", "taken", "out"))
    landed = [m.dma_sem(f"{name}_landed{s}") for s in range(2)]
    rows = [m.rows[s][:, :, 0:D] for s in range(2)]
    ps = [m.psum[s][:, 0:D] for s in range(2)]
    nrec = ET * 3

    @block.vector
    def _(dve):
        def stage(c, s, first):
            nc.vector.tensor_scalar(m.stage[s][:, :, :].rearrange("p t k -> p (t k)"), rec[:, bass.ds(c * nrec, nrec)], 0.0, None, ALU.add).then_inc(copied, 1)
            dve.wait_ge(copied, c + 1)
            nc.vector.tensor_copy(m.stage_idx[s][:, :], m.stage[s][:, :, 1]).then_inc(staged, 1)
            for t in range(ET):
                ins = nc.vector.tensor_scalar(m.hot[s][:, t, :], m.iota[:, :], m.stage[s][:, t, 0:1], m.stage[s][:, t, 2:3],
                                              ALU.is_equal, ALU.mult)
            ins.then_inc(hot, 1)

        def take(c, s):
            b = dve.value_load(bucket[0:1, bass.ds(c, 1)], min_val=0, max_val=NT)
            dve.wait_ge(summed, c + 1)
            dve.wait_ge(taken, c + 1)
            nc.vector.tensor_tensor(m.acc[:, b, 0:D], m.acc[:, b, 0:D], ps[s], ALU.add).then_inc(taken, 1)

        dve.sem_inc(taken, 1)
        nc.vector.memset(m.acc[:, :, :], 0.0).then_inc(out, 1)
        dve.wait_ge(out, 1)
        for s in range(2):
            stage(s, s, True)
        with dve.Fori(0, nch // 2 - 1) as i:
            for s in range(2):
                take(i * 2 + s, s)
                stage(i * 2 + (2 + s), s, False)
        for s in range(2):
            take(nch - 2 + s, s)

    @block.gpsimd
    def _(pool):
        with pool.Fori(0, nch // 2) as i:
            for s in range(2):
                pool.wait_ge(staged, i * 2 + s + 1)
                pool.sem_inc(passed, 1)
                for t in range(ET):
                    nc.gpsimd.indirect_dma_start(
                        out=rows[s][:, t, :], out_offset=None, in_=table,
                        in_offset=bass.IndirectOffsetOnAxis(ap=m.stage_idx[s][:, t:t + 1], axis=0)).then_inc(landed[s], 16)

    @block.tensor
    def _(pe):
        with pe.Fori(0, nch // 2) as i:
            for s in range(2):
                pe.wait_ge(hot, i * 2 + s + 1)
                pe.wait_ge(landed[s], i * (16 * ET) + 16 * ET)
                for t in range(ET):
                    ins = nc.tensor.matmul(ps[s], m.hot[s][:, t, :], rows[s][:, t, :], start=t == 0, stop=t == ET - 1)
                ins.then_inc(summed, 1)


def attend_edges(nc, block, m, name, width, table, rec, bucket, nch):
    dh = width // HEADS
    w1 = dh + 1
    hw = HEADS * w1
    rw = hw + HEADS
    nrec = ET * 3
    SL = 3
    s_ = lambda n: m.sem(f"{name}_{n}")
    passed, copied, staged, hot, pen_r, hott, hott_sb, best, best_t, top, spread, score, wexp, shrink, scaled, summed, taken, chain_s = (
        s_(n) for n in ("passed", "copied", "staged", "hot", "pen", "hott", "hottsb", "best", "bestt", "top", "spread", "score", "wexp",
                        "shrink", "scaled", "summed", "taken", "chain"))
    landed = [m.dma_sem(f"{name}_landed{s}") for s in range(SL)]
    rows = [m.rows[s][:, :, 0:rw] for s in range(SL)]
    ps_hott, ps_best, ps_spread = m.psum[0], m.psum[1], m.psum[2]
    ps_sum = [m.psum[3 + s][:, 0:hw] for s in range(2)]
    trips = nch // 6

    @block.gpsimd
    def _(pool):
        with pool.Fori(0, nch // SL) as i:
            for s in range(SL):
                pool.wait_ge(staged, i * SL + s + 1)
                pool.sem_inc(passed, 1)
                for t in range(ET):
                    nc.gpsimd.indirect_dma_start(
                        out=rows[s][:, t, :], out_offset=None, in_=table,
                        in_offset=bass.IndirectOffsetOnAxis(ap=m.stage_idx[s][:, t:t + 1], axis=0)).then_inc(landed[s], 16)

    @block.vector
    def _(dve):
        chain = Chain(dve, chain_s)

        def stage(c, s):
            nc.vector.tensor_scalar(m.stage[s][:, :, :].rearrange("p t k -> p (t k)"), rec[:, bass.ds(c * nrec, nrec)], 0.0, None, ALU.add).then_inc(copied, 1)
            dve.wait_ge(copied, c + 1)
            nc.vector.tensor_copy(m.stage_idx[s][:, :], m.stage[s][:, :, 1]).then_inc(staged, 1)
            nc.vector.tensor_tensor(m.hot[s][:, :, :], m.iota[:, :].unsqueeze(1).to_broadcast([P, ET, P]),
                                    m.stage[s][:, :, 0:1].to_broadcast([P, ET, P]), ALU.is_equal).then_inc(hot, 1)

        def maximum(c, s, i3, z):
            dve.wait_ge(landed[s], i3 * (16 * ET) + 16 * ET)
            dve.wait_ge(pen_r, c + 1)
            dve.wait_ge(best_t, c)
            for t in range(ET):
                for h in range(HEADS):
                    a = rows[s][:, t, hw + h:hw + h + 1]
                    if t == 0:
                        ins = nc.vector.tensor_scalar(m.best[:, h, :], m.pen[z][:, t, :], a, None, ALU.add)
                    else:
                        ins = nc.vector.scalar_tensor_tensor(m.best[:, h, :], m.pen[z][:, t, :], a, m.best[:, h, :], ALU.add, ALU.max)
                if t < ET - 1:
                    chain.next(ins)
                else:
                    ins.then_inc(best, 1)

        def load_bucket(c):
            return dve.value_load(bucket[0:1, bass.ds(c, 1)], min_val=0, max_val=NT)

        def raise_top(b, c, z):
            st, am = m.state[:, b, :], m.acc[:, b, hw:rw]
            adm, drop, sm = m.adm[z], m.drop[z], m.small
            dve.wait_ge(best_t, c + 1)
            chain.next(nc.vector.tensor_reduce(sm[:, 0:4], ps_best[:, :].rearrange("p (h e) -> p h e", h=HEADS), AX.X, ALU.max))
            chain.next(nc.vector.tensor_tensor(am, am, sm[:, 0:4], ALU.max))
            chain.next(nc.vector.tensor_tensor(sm[:, 4:8], am, st[:, 0:HEADS], ALU.add))
            nc.vector.tensor_scalar(adm[:, 0:4], st[:, 0:HEADS], 0.0, None, ALU.add)
            chain.next(nc.vector.scalar_tensor_tensor(adm[:, 4:8], sm[:, 4:8], 0.2, sm[:, 4:8], ALU.mult, ALU.max))
            nc.vector.tensor_tensor(drop[:, :], st[:, HEADS:2 * HEADS], adm[:, 4:8], ALU.subtract).then_inc(top, 1)
            dve.wait_ge(top, c + 1)
            chain.next(nc.vector.tensor_scalar(st[:, HEADS:2 * HEADS], adm[:, 4:8], 0.0, None, ALU.add))

        def scores(c, s, z):
            sc = m.score[z]
            dve.wait_ge(spread, c + 1)
            sp = ps_spread[:, 0:8 * ET].rearrange("p (t k) -> p t k", t=ET)
            v = sc[:, :].rearrange("p (t h) -> p t h", t=ET)
            chain.next(nc.vector.tensor_tensor(v, rows[s][:, :, hw:rw], sp[:, :, 0:4], ALU.add))
            chain.next(nc.vector.scalar_tensor_tensor(sc[:, :], sc[:, :], 0.2, sc[:, :], ALU.mult, ALU.max))
            chain.next(nc.vector.tensor_tensor(v, v, sp[:, :, 4:8], ALU.subtract))
            nc.vector.tensor_scalar(sc[:, :], sc[:, :], 0.0, None, ALU.min).then_inc(score, 1)

        def scale(c, s, z):
            dve.wait_ge(wexp, c + 1)
            nc.vector.tensor_tensor(
                m.msg[z][:, 0:ET * hw].rearrange("p (t h w) -> p t h w", t=ET, h=HEADS),
                rows[s][:, :, 0:hw].rearrange("p t (h w) -> p t h w", h=HEADS),
                m.wexp[z][:, :].rearrange("p (t h) -> p t h", t=ET).unsqueeze(3).to_broadcast([P, ET, HEADS, w1]),
                ALU.mult).then_inc(scaled, 1)

        def take(b, c, z):
            acc = m.acc[:, b, 0:hw]
            dve.wait_ge(shrink, c + 1)
            chain.next(nc.vector.tensor_tensor(acc.rearrange("p (h w) -> p h w", h=HEADS), acc.rearrange("p (h w) -> p h w", h=HEADS),
                                               m.fac[z][:, :].unsqueeze(2).to_broadcast([P, HEADS, w1]), ALU.mult))
            dve.wait_ge(summed, c + 1)
            nc.vector.tensor_tensor(acc, acc, ps_sum[z], ALU.add).then_inc(taken, 1)
            dve.wait_ge(taken, c + 1)

        def body(c, k, i3, first=False, last2=False, last=False):
            s, z = k % 3, k % 2
            b = load_bucket(c)
            b_before = None if first else load_bucket(c + (-1))
            raise_top(b, c, z)
            if not first:
                take(b_before, c + (-1), 1 - z)
            if not last:
                maximum(c + 1, (s + 1) % 3, i3 + (1 if s == 2 else 0), 1 - z)
            scores(c, s, z)
            if not (last or last2):
                stage(c + 2, (s + 2) % 3)
            scale(c, s, z)

        nc.vector.memset(m.acc[:, NT, :], 0.0)
        chain.next(nc.vector.memset(m.state[:, NT, :], 0.0))
        stage(0, 0)
        stage(1, 1)
        maximum(0, 0, 0, 0)
        for k in range(6):
            body(k, k, k // 3, first=k == 0)
        per = 3 + 5 + 3 + 1
        with dve.Fori(0, trips - 2) as i:
            chain.enter(i, 6 * per)
            for k in range(6):
                body(i * 6 + (6 + k), k, i * 2 + (2 + k // 3))
        chain.leave(trips - 2)
        for k in range(6):
            c = nch - 6 + k
            body(c, k, c // 3, last2=k == 4, last=k == 5)
        take(load_bucket(nch - 1), nch - 1, (nch - 1) % 2)

    @block.scalar
    def _(act):
        def front(c, s, z):
            act.wait_ge(hot, c + 1)
            act.wait_ge(best, c + (-1) if not isinstance(c, int) else max(c - 1, 0))
            nc.scalar.activation(m.pen[z][:, :, :], m.hot[s][:, :, :], ACT.Copy, bias=-BIG, scale=BIG).then_inc(pen_r, 1)
            act.wait_ge(hott, c + 1)
            nc.scalar.copy(m.hott[z][:, :, :].rearrange("p t e -> p (t e)"), ps_hott[:, :]).then_inc(hott_sb, 1)

        def back(c, z):
            act.wait_ge(top, c + 1)
            nc.scalar.activation(m.fac[z][:, :], m.drop[z][:, :], ACT.Exp).then_inc(shrink, 1)
            act.wait_ge(score, c + 1)
            nc.scalar.activation(m.wexp[z][:, :], m.score[z][:, :], ACT.Exp).then_inc(wexp, 1)

        front(0, 0, 0)
        front(1, 1, 1)
        for k in range(6):
            back(k, k % 2)
            front(k + 2, (k + 2) % 3, k % 2)
        with act.Fori(0, trips - 2) as i:
            for k in range(6):
                back(i * 6 + (6 + k), k % 2)
                front(i * 6 + (8 + k), (k + 2) % 3, k % 2)
        for k in range(6):
            c = nch - 6 + k
            back(c, k % 2)
            if k < 4:
                front(c + 2, (k + 2) % 3, k % 2)

    @block.tensor
    def _(pe):
        def turn_hot(c, s):
            pe.wait_ge(hot, c + 1)
            pe.wait_ge(hott_sb, c)
            for t in range(ET):
                ins = nc.tensor.transpose(ps_hott[:, t * P:(t + 1) * P], m.hot[s][:, t, :], m.ident[:, :])
            ins.then_inc(hott, 1)

        def turn_best(c):
            pe.wait_ge(best, c + 1)
            pe.wait_ge(top, c)
            for h in range(HEADS):
                ins = nc.tensor.transpose(ps_best[:, h * P:(h + 1) * P], m.best[:, h, :], m.ident[:, :])
            ins.then_inc(best_t, 1)

        def spread_top(c, z):
            pe.wait_ge(top, c + 1)
            pe.wait_ge(hott_sb, c + 1)
            for t in range(ET):
                ins = nc.tensor.matmul(ps_spread[:, 8 * t:8 * t + 8], m.hott[z][:, t, :], m.adm[z][:, :], start=True, stop=True)
            ins.then_inc(spread, 1)

        def sums(c, s, z):
            pe.wait_ge(scaled, c + 1)
            if not isinstance(c, int) or c >= 2:
                pe.wait_ge(taken, c + (-1))
            for t in range(ET):
                ins = nc.tensor.matmul(ps_sum[z], m.hot[s][:, t, :], m.msg[z][:, t * hw:(t + 1) * hw], start=t == 0, stop=t == ET - 1)
            ins.then_inc(summed, 1)

        def body(c, k, last2=False, last=False):
            s, z = k % 3, k % 2
            spread_top(c, z)
            if not last:
                turn_best(c + 1)
            if not (last or last2):
                turn_hot(c + 2, (s + 2) % 3)
            sums(c, s, z)

        turn_hot(0, 0)
        turn_hot(1, 1)
        turn_best(0)
        for k in range(6):
            body(k, k)
        with pe.Fori(0, trips - 2) as i:
            for k in range(6):
                body(i * 6 + (6 + k), k)
        for k in range(6):
            body(nch - 6 + k, k, last2=k == 4, last=k == 5)



def add_sums(nc, block, m, name, bias_in):
    loaded, steps = m.sem(f"{name}_loaded"), m.sem(f"{name}_steps")

    @block.sync
    def _(sp):
        sp.dma_start(m.bias[:, :], bias_in.partition_broadcast(P)).then_inc(loaded, 16)

    @block.vector
    def _(dve):
        chain = Chain(dve, steps)
        chain.next(nc.vector.tensor_tensor(m.x[:, :, :], m.x[:, :, :], m.acc[:, 0:NT, 0:D], ALU.add))
        dve.wait_ge(loaded, 16)
        chain.next(nc.vector.tensor_tensor(m.x[:, :, :], m.x[:, :, :], m.bias[:, :].unsqueeze(1).to_broadcast([P, NT, D]), ALU.add))


def attended(nc, m, chain, width, out):
    dh = width // HEADS
    acc = m.acc[:, 0:NT, 0:width + HEADS].rearrange("p t (h w) -> p t h w", h=HEADS)
    den = m.den[:, :, :]
    chain.next(nc.vector.tensor_scalar(den, acc[:, :, :, dh], 1e-16, None, ALU.add))
    chain.next(nc.vector.reciprocal(den, den))
    chain.next(nc.vector.tensor_tensor(out.rearrange("p t (h c) -> p t h c", h=HEADS), acc[:, :, :, 0:dh],
                                       den.unsqueeze(3).to_broadcast([P, NT, HEADS, dh]), ALU.mult))


def finish_layer(nc, block, m, name, layer, bias_in):
    loaded, steps = m.sem(f"{name}_loaded"), m.sem(f"{name}_steps")
    xt = m.hidden

    @block.sync
    def _(sp):
        sp.dma_start(m.bias[:, :], bias_in.partition_broadcast(P)).then_inc(loaded, 16)

    @block.vector
    def _(dve):
        chain = Chain(dve, steps)
        attended(nc, m, chain, D, xt)
        dve.wait_ge(loaded, 16)
        chain.next(nc.vector.tensor_tensor(xt, xt, m.bias[:, :].unsqueeze(1).to_broadcast([P, NT, D]), ALU.add))
        if layer == 0:
            chain.next(nc.vector.scalar_tensor_tensor(xt, xt, 0.0, m.xn[:, :, :], ALU.max, ALU.add))
        elif layer == 1:
            chain.next(nc.vector.tensor_scalar(xt, xt, 0.0, None, ALU.max))
        else:
            chain.next(nc.vector.tensor_tensor(xt, xt, m.xn[:, :, :], ALU.add))
            chain.next(nc.vector.scalar_tensor_tensor(m.x[:, :, :], xt, 0.0, m.x[:, :, :], ALU.max, ALU.add))


def gate_nodes(nc, block, m, name, b_in, gamma_in, beta_in):
    NE = 4
    loaded, steps, var_ready, std_ready, to_exp, exped = (m.sem(f"{name}_{s}") for s in ("loaded", "steps", "var", "std", "toexp", "exped"))
    W = 16
    at = [0]

    def take(*shape):
        n = 1
        for d in shape:
            n *= d
        v = m.work[:, at[0]:at[0] + n]
        at[0] += n
        return v

    agg = take(NT * W).rearrange("p (t c) -> p t c", t=NT)
    sq = take(NT * W).rearrange("p (t c) -> p t c", t=NT)
    mean, var, std, top, tot = (take(NT) for _ in range(5))
    sc = take(NT * NE).rearrange("p (t e) -> p t e", t=NT)
    rank = take(NT * NE).rearrange("p (t e) -> p t e", t=NT)
    gt = take(NT * NE * NE).rearrange("p (t i j) -> p t i j", t=NT, i=NE)
    eq = take(NT * NE * NE).rearrange("p (t i j) -> p t i j", t=NT, i=NE)

    def wide(a, w=W):
        return a.unsqueeze(2).to_broadcast([P, NT, w])

    def par(k):
        return m.bias[:, k * W:(k + 1) * W].unsqueeze(1).to_broadcast([P, NT, W])

    @block.sync
    def _(sp):
        for k, a in enumerate((b_in, gamma_in, beta_in)):
            sp.dma_start(m.bias[:, k * W:(k + 1) * W], a.partition_broadcast(P)).then_inc(loaded, 16)

    @block.vector
    def _(dve):
        chain = Chain(dve, steps)
        attended(nc, m, chain, W, agg)
        dve.wait_ge(loaded, 48)
        chain.next(nc.vector.tensor_tensor(agg, agg, par(0), ALU.add))
        chain.next(nc.vector.tensor_reduce(mean, agg, AX.X, ALU.add))
        chain.next(nc.vector.tensor_scalar(mean, mean, 1.0 / W, None, ALU.mult))
        chain.next(nc.vector.tensor_tensor(agg, agg, wide(mean), ALU.subtract))
        chain.next(nc.vector.tensor_tensor(sq, agg, agg, ALU.mult))
        chain.next(nc.vector.tensor_reduce(var, sq, AX.X, ALU.add))
        nc.vector.tensor_scalar(var, var, 1.0 / W, LN_EPS, ALU.mult, ALU.add).then_inc(var_ready, 1)
        dve.wait_ge(std_ready, 1)
        chain.next(nc.vector.reciprocal(std, std))
        chain.next(nc.vector.tensor_tensor(agg, agg, wide(std), ALU.mult))
        chain.next(nc.vector.tensor_tensor(agg, agg, par(1), ALU.mult))
        chain.next(nc.vector.tensor_tensor(agg, agg, par(2), ALU.add))
        chain.next(nc.vector.tensor_reduce(sc, agg.rearrange("p t (h e) -> p t e h", h=HEADS), AX.X, ALU.add))
        chain.next(nc.vector.tensor_scalar(sc, sc, 1.0 / HEADS, None, ALU.mult))
        rank_of(nc, m, chain, sc, gt, eq, rank, NE, NT)
        chain.next(nc.vector.tensor_reduce(top, sc, AX.X, ALU.max))
        nc.vector.tensor_tensor(sc, sc, wide(top, NE), ALU.subtract).then_inc(to_exp, 1)
        chain.next(nc.vector.tensor_scalar(rank, rank, 2.0, None, ALU.is_lt))
        dve.wait_ge(exped, 1)
        chain.next(nc.vector.tensor_tensor(sc, sc, rank, ALU.mult))
        chain.next(nc.vector.tensor_reduce(tot, sc, AX.X, ALU.add))
        chain.next(nc.vector.reciprocal(tot, tot))
        chain.next(nc.vector.tensor_tensor(m.gates[:, :, :].rearrange("p e t -> p t e"), sc, wide(tot, NE), ALU.mult))

    @block.scalar
    def _(act):
        act.wait_ge(var_ready, 1)
        nc.scalar.activation(std, var, ACT.Sqrt).then_inc(std_ready, 1)
        act.wait_ge(to_exp, 1)
        nc.scalar.activation(sc, sc, ACT.Exp).then_inc(exped, 1)


def rank_of(nc, m, chain, sc, gt, eq, rank, ne, nt):
    at_j = sc.unsqueeze(2).to_broadcast([P, nt, ne, ne])
    at_i = sc.unsqueeze(3).to_broadcast([P, nt, ne, ne])
    chain.next(nc.vector.tensor_tensor(gt, at_j, at_i, ALU.is_gt))
    chain.next(nc.vector.tensor_tensor(eq, at_j, at_i, ALU.is_equal))
    chain.next(nc.vector.tensor_tensor(eq, eq, m.lower[:, 0:ne, 0:ne].unsqueeze(1).to_broadcast([P, nt, ne, ne]), ALU.mult))
    chain.next(nc.vector.tensor_tensor(gt, gt, eq, ALU.add))
    chain.next(nc.vector.tensor_reduce(rank, gt, AX.X, ALU.add))


def turn_rows(nc, block, m, name):
    staged, turned, out = m.sem(f"{name}_staged"), m.sem(f"{name}_turned"), m.sem(f"{name}_out")
    ps_t = [m.psum[j][:, 0:2 * P].rearrange("p (k n) -> p k n", k=2) for j in range(GN)]

    @block.scalar
    def _(act):
        act.sem_inc(out, 1)
        with act.Fori(0, NT // GN) as i:
            for j in range(GN):
                act.wait_ge(turned, i * GN + 1)
                nc.scalar.copy(m.slot_x[j][:, :], m.xn[:, i * GN + j, :]).then_inc(staged, 1)
            for j in range(GN):
                act.wait_ge(turned, i * GN + j + 2)
                nc.scalar.copy(m.xt[:, :, bass.ds(i * (GN * P) + j * P, P)], ps_t[j]).then_inc(out, 1)

    @block.tensor
    def _(pe):
        pe.sem_inc(turned, 1)
        with pe.Fori(0, NT // GN) as i:
            for j in range(GN):
                pe.wait_ge(staged, i * GN + j + 1)
                pe.wait_ge(out, i * GN + 1)
                for k in range(2):
                    ins = nc.tensor.transpose(ps_t[j][:, k, :], m.slot_x[j][:, k * P:(k + 1) * P], m.ident[:, :])
                ins.then_inc(turned, 1)


def route(nc, block, m, name, wr_in, br_in, w1_in, b1_in, w2_in, b2_in):
    NE = 8
    capacity = float(-(-int(N * 1.25) // NE))
    assert capacity == 489.0
    loaded, steps, summed, mean_in, logits_in, e1, e1d, e2, e2d, e3, e3d, index, wide_in = (
        m.sem(f"{name}_{s}") for s in ("loaded", "steps", "summed", "mean", "logits", "e1", "e1d", "e2", "e2d", "e3", "e3d",
                                       "index", "wide"))
    got = m.dma_sem(f"{name}_got")
    work = m.work
    colsum = work[:, 12000:12000 + D]
    mu = work[:, 12256:12258]
    muw = work[:, 12300:12300 + 2 * P].rearrange("p (k n) -> p k n", k=2)
    wr = work[:, 12600:12600 + 2 * NE].rearrange("p (k e) -> p k e", k=2)
    br = work[:, 12620:12620 + NE]
    rw, ex, scl = work[:, 12640:12648], work[:, 12650:12658], work[:, 12660:12668]
    top, tot = work[:, 12670:12671], work[:, 12671:12672]
    gt = work[:, 12700:12764].rearrange("p (t i j) -> p t i j", t=1, i=NE)
    eq = work[:, 12764:12828].rearrange("p (t i j) -> p t i j", t=1, i=NE)
    rank = work[:, 12830:12838]
    sel, val, num = work[:, 12840:12848], work[:, 12850:12852], work[:, 12852:12854]
    diff = work[:, 12854:12855]
    ps_mean, ps_logit = m.psum[6][:, 0:2], m.psum[7][:, 0:NE]
    offs = work[:, 12860:12874]
    offs_i = m.expert_rows

    @block.sync
    def _(sp):
        sp.dma_start(wr, wr_in.rearrange("(k p) e -> p k e", p=P)).then_inc(loaded, 16)
        sp.dma_start(br, br_in.partition_broadcast(P)).then_inc(loaded, 16)

    @block.tensor
    def _(pe):
        pe.wait_ge(summed, 1)
        for k in range(2):
            nc.tensor.matmul(ps_mean[:, k:k + 1], colsum[:, k * P:(k + 1) * P], m.ones[:, 0:1], start=True, stop=False)
            ins = nc.tensor.matmul(ps_mean[:, k:k + 1], m.xn[0:LAST, NT - 1, k * P:(k + 1) * P], m.ones[0:LAST, 0:1], start=False, stop=True)
        ins.then_inc(mean_in, 1)
        pe.wait_ge(wide_in, 1)
        pe.wait_ge(loaded, 32)
        for k in range(2):
            ins = nc.tensor.matmul(ps_logit, muw[:, k, :], wr[:, k, :], start=k == 0, stop=k == 1)
        ins.then_inc(logits_in, 1)

    @block.vector
    def _(dve):
        chain = Chain(dve, steps)
        nc.vector.tensor_reduce(colsum, m.xn[:, 0:NT - 1, :].rearrange("p t d -> p d t"), AX.X, ALU.add).then_inc(summed, 1)
        dve.wait_ge(mean_in, 1)
        chain.next(nc.vector.tensor_scalar(mu, ps_mean, 1.0 / N, None, ALU.mult))
        nc.vector.tensor_copy(muw, mu.unsqueeze(2).to_broadcast([P, 2, P])).then_inc(wide_in, 1)
        dve.wait_ge(logits_in, 1)
        chain.next(nc.vector.tensor_tensor(rw, ps_logit, br, ALU.add))
        for n, (ready, done) in enumerate(((e1, e1d), (e2, e2d))):
            chain.next(nc.vector.tensor_reduce(top, rw, AX.X, ALU.max))
            nc.vector.tensor_scalar(rw, rw, top, None, ALU.subtract).then_inc(ready, 1)
            dve.wait_ge(done, 1)
            chain.next(nc.vector.tensor_reduce(tot, ex, AX.X, ALU.add))
            chain.next(nc.vector.reciprocal(tot, tot))
            chain.next(nc.vector.tensor_scalar(rw, ex, tot, None, ALU.mult))
            if n == 0:
                chain.next(nc.vector.tensor_scalar(scl, rw, float(N), 1e-30, ALU.mult, ALU.max))
                chain.next(nc.vector.reciprocal(scl, scl))
                chain.next(nc.vector.tensor_scalar(scl, scl, capacity, 1.0, ALU.mult, ALU.min))
                chain.next(nc.vector.tensor_tensor(rw, rw, scl, ALU.mult))
        rank_of(nc, m, chain, rw.unsqueeze(1), gt, eq, rank.unsqueeze(1), NE, 1)
        for k in range(2):
            chain.next(nc.vector.tensor_scalar(sel, rank, float(k), None, ALU.is_equal))
            chain.next(nc.vector.tensor_tensor(ex, sel, rw, ALU.mult))
            chain.next(nc.vector.tensor_reduce(val[:, k:k + 1], ex, AX.X, ALU.add))
            chain.next(nc.vector.tensor_tensor(ex, sel, m.iota[:, 0:NE], ALU.mult))
            chain.next(nc.vector.tensor_reduce(num[:, k:k + 1], ex, AX.X, ALU.add))
        nc.vector.tensor_tensor(diff, val[:, 1:2], val[:, 0:1], ALU.subtract).then_inc(e3, 1)
        dve.wait_ge(e3d, 1)
        chain.next(nc.vector.tensor_scalar(tot, diff, 1.0, None, ALU.add))
        chain.next(nc.vector.reciprocal(tot, tot))
        chain.next(nc.vector.tensor_copy(m.gates[:, 0, :], tot.to_broadcast([P, NT])))
        chain.next(nc.vector.tensor_tensor(tot, tot, diff, ALU.mult))
        chain.next(nc.vector.tensor_copy(m.gates[:, 1, :], tot.to_broadcast([P, NT])))
        for k in range(2):
            for c in range(2):
                chain.next(nc.vector.tensor_scalar(offs[:, 7 * k + c:7 * k + c + 1], num[:, k:k + 1], float(D), float(c * P), ALU.mult, ALU.add))
            for c in range(4):
                chain.next(nc.vector.tensor_scalar(offs[:, 7 * k + 2 + c:7 * k + 3 + c], num[:, k:k + 1], float(F), float(c * P), ALU.mult, ALU.add))
            chain.next(nc.vector.tensor_tensor(offs[:, 7 * k:7 * k + 6], offs[:, 7 * k:7 * k + 6], m.pid[:, 0:1].to_broadcast([P, 6]), ALU.add))
            chain.next(nc.vector.tensor_copy(offs[:, 7 * k + 6:7 * k + 7], num[:, k:k + 1]))
        nc.vector.tensor_copy(offs_i[:, :], offs).then_inc(index, 1)

    @block.scalar
    def _(act):
        for ready, done in ((e1, e1d), (e2, e2d)):
            act.wait_ge(ready, 1)
            nc.scalar.activation(ex, rw, ACT.Exp).then_inc(done, 1)
        act.wait_ge(e3, 1)
        nc.scalar.activation(diff, diff, ACT.Exp).then_inc(e3d, 1)

    @block.gpsimd
    def _(pool):
        def gather(out, table, col):
            nc.gpsimd.indirect_dma_start(out=out, out_offset=None, in_=table,
                                         in_offset=bass.IndirectOffsetOnAxis(ap=offs_i[:, col:col + 1], axis=0)).then_inc(got, 16)

        pool.wait_ge(index, 1)
        for k in range(2):
            for c in range(2):
                gather(m.w1[k][:, c, :], w1_in.rearrange("e d f -> (e d) f"), 7 * k + c)
            for c in range(4):
                gather(m.w2[k][:, c, :], w2_in.rearrange("e f d -> (e f) d"), 7 * k + 2 + c)
                gather(m.b1[k][:, c:c + 1], b1_in.rearrange("e (f o) -> (e f) o", o=1), 7 * k + 2 + c)
            gather(m.b2[k][:, :], b2_in, 7 * k + 6)
        pool.wait_ge(got, 2 * 11 * 16)


def experts(nc, block, m, name, ne, out, params=None):
    loaded = [m.sem(f"{name}_loaded{s}") for s in range(2)]
    hidden, gelud, made, added = (m.sem(f"{name}_{s}") for s in ("hidden", "gelud", "made", "added"))
    half = GN * P // 2
    ps_h = [m.psum_all[:, 2 * b:2 * b + 2, 0:half] for b in range(2)]
    ps_y = [m.psum[4 + j % 4][:, 0:D] for j in range(GN)]
    trips = NT // GN
    KF = F // P
    ht = m.work[:, 0:KF * GN * P].rearrange("p (k n) -> p k n", k=KF)


    @block.sync
    def _(sp):
        if params is not None:
            w1_in, b1_in, w2_in, b2_in = params
            for e in range(ne):
                s = e % 2
                if e >= 2:
                    sp.wait_ge(made, NT * (e - 1) + 1)
                sp.dma_start(m.w1[s][:, :, :], w1_in[e].rearrange("(k p) f -> p k f", p=P)).then_inc(loaded[s], 16)
                sp.dma_start(m.w2[s][:, :, :], w2_in[e].rearrange("(k p) d -> p k d", p=P)).then_inc(loaded[s], 16)
                with nc.allow_non_contiguous_dma(reason="512 biases to the partitions of their features"):
                    sp.dma_start(m.b1[s][:, :], b1_in[e].rearrange("(k p) -> p k", p=P)).then_inc(loaded[s], 16)
                sp.dma_start(m.b2[s][0:1, :], b2_in[e:e + 1, :]).then_inc(loaded[s], 16)

    @block.tensor
    def _(pe):
        pe.sem_inc(made, 1)
        for e in range(ne):
            s = e % 2
            if params is not None:
                pe.wait_ge(loaded[s], 64 * (e // 2 + 1))
            w1, w2, b2 = m.w1[s], m.w2[s], m.b2[s]
            with pe.Fori(0, trips) as i:
                for f in range(KF):
                    pe.wait_ge(gelud, i * KF + (e * trips * KF + f + 1))
                    for k in range(2):
                        for hf in range(2):
                            ins = nc.tensor.matmul(ps_h[f % 2][:, hf, :], w1[:, k, f * P:(f + 1) * P],
                                                   m.xt[:, k, bass.ds(i * (GN * P) + hf * half, half)], start=k == 0, stop=k == 1)
                    ins.then_inc(hidden, 1)
                pe.wait_ge(gelud, i * KF + (e * trips * KF + KF + 2))
                pe.wait_ge(added, i * GN + (e * NT + 1))
                for j in range(GN):
                    if j >= 4:
                        pe.wait_ge(added, i * GN + (e * NT + j - 2))
                    for k in range(KF):
                        nc.tensor.matmul(ps_y[j], ht[:, k, j * P:(j + 1) * P], w2[:, k, :], start=k == 0, stop=False)
                    nc.tensor.matmul(ps_y[j], m.ones[0:1, :], b2[0:1, :], start=False, stop=True).then_inc(made, 1)

    @block.scalar
    def _(act):
        act.sem_inc(gelud, 2)
        for e in range(ne):
            if params is not None:
                act.wait_ge(loaded[e % 2], 64 * (e // 2 + 1))
            with act.Fori(0, trips) as i:
                for f in range(KF):
                    act.wait_ge(hidden, i * KF + (e * trips * KF + f + 1))
                    act.wait_ge(made, i * GN + (e * NT + 1))
                    nc.scalar.activation(ht[:, f, :].rearrange("p (a n) -> p a n", a=2), ps_h[f % 2], ACT.Gelu,
                                         bias=m.b1[e % 2][:, f:f + 1]).then_inc(gelud, 1)

    @block.vector
    def _(dve):
        dve.sem_inc(added, 1)
        for e in range(ne):
            with dve.Fori(0, trips) as i:
                for j in range(GN):
                    t = i * GN + j
                    dve.wait_ge(made, i * GN + (e * NT + j + 2))
                    if e:
                        dve.wait_ge(added, i * GN + (e * NT + j - NT + 2))
                    nc.vector.scalar_tensor_tensor(out[:, t, :], ps_y[j], m.gates[:, e, bass.ds(t, 1)], out[:, t, :],
                                                   ALU.mult, ALU.add).then_inc(added, 1)


def finish(nc, block, m, gamma_in, beta_in, y_out):
    loaded, steps, made, stored = m.sem("fin_loaded"), m.sem("fin_steps"), m.sem("fin_made"), m.sem("fin_stored")

    @block.sync
    def _(sp):
        sp.dma_start(m.bias[:, :], gamma_in.partition_broadcast(P)).then_inc(loaded, 16)
        sp.dma_start(m.prod[:, 0, :], beta_in.partition_broadcast(P)).then_inc(loaded, 16)
        sp.wait_ge(made, 1)
        sp.dma_start(y_out[0:(NT - 1) * P, :].rearrange("(t p) d -> p t d", p=P), m.xn[:, 0:NT - 1, :]).then_inc(stored, 16)
        sp.dma_start(y_out[(NT - 1) * P:N, :], m.xn[0:LAST, NT - 1, :]).then_inc(stored, 16)
        sp.wait_ge(stored, 32)

    @block.vector
    def _(dve):
        chain = Chain(dve, steps)
        dve.wait_ge(loaded, 32)
        chain.next(nc.vector.tensor_tensor(m.x[:, :, :], m.x[:, :, :], m.prod[:, 0, :].unsqueeze(1).to_broadcast([P, NT, D]), ALU.add))
        chain.next(nc.vector.tensor_tensor(m.xn[:, :, :], m.xn[:, :, :], m.bias[:, :].unsqueeze(1).to_broadcast([P, NT, D]), ALU.mult))
        nc.vector.tensor_tensor(m.xn[:, :, :], m.xn[:, :, :], m.x[:, :, :], ALU.add).then_inc(made, 1)



class Memory:

    turn = 0
    semaphores = None


def memory(nc, ctx):
    m = Memory()

    def sb(name, shape, dt=F32):
        return ctx.enter_context(nc.sbuf_tensor(name, shape, dt))

    m.dma_sem = lambda name: ctx.enter_context(nc.semaphore(name))
    m.x = sb("x", [P, NT, D])
    m.xn = sb("xn", [P, NT, D])
    m.xt = sb("xt", [P, 2, NT * P])
    m.hidden = m.xt[:, :, :].rearrange("p k n -> p (k n)").rearrange("p (t d) -> p t d", t=NT)
    m.acc = sb("acc", [P, NT + 1, D + 2 * HEADS])
    m.state = sb("state", [P, NT + 1, 2 * HEADS])
    m.den = sb("den", [P, NT, HEADS])
    m.work = sb("work", [P, 15000])
    m.rec = [sb(f"rec{k}", [P, n * ET * 3]) for k, n in enumerate((NCH, NCHG, NCH))]
    m.bucket = [sb(f"bucket{k}", [P, n], I32) for k, n in enumerate((NCH, NCHG, NCH))]
    flat = m.xt[:, :, :].rearrange("p k n -> p (k n)")
    cols = [flat[:, 400 * k:400 * (k + 1)] for k in range(10)]
    m.sort_key, m.sort_val, m.sort_lo, m.sort_place, m.sort_row = (c.bitcast(I32) for c in cols[0:5])
    m.sort_hi, m.sort_w, m.sort_hi2, m.sort_lo_f, m.sort_val_f = cols[5:10]
    m.sort_small = flat[:, 4000:4000 + 8 * 32].rearrange("p (k n) -> p k n", k=8)
    m.sort_small_i = flat[:, 4300:4300 + NT].bitcast(I32)
    m.stage_rec = [sb(f"stage_rec{s}", [P, COPIES // 2, 3]) for s in range(2)]
    m.stage_row = [sb(f"stage_row{s}", [P, COPIES // 2], I32) for s in range(2)]
    m.ident, m.before, m.ones, m.iota = (sb(n, [P, P]) for n in ("ident", "before", "ones", "iota"))
    m.iota_i = m.work[:, 0:P].bitcast(I32)
    m.iota_c = m.work[:, P:P + NCH].bitcast(I32)
    m.pid_i = m.work[:, 300:302].bitcast(I32)
    m.iotac, m.pid, m.dummy, m.lower = sb("iotac", [P, NCH]), sb("pid", [P, 2]), sb("dummy_rows", [P, 2]), sb("lower", [P, 8, 8])
    m.stats = sb("stats", [P, 3, NT])
    m.bias, m.prod, m.att = sb("bias", [P, D]), sb("prod", [P, 2, D]), sb("att", [P, 2, D])
    m.small, m.idle = sb("small", [P, 16]), sb("idle", [P, 1])
    m.gates = sb("gates", [P, 4, NT])
    m.expert_rows = sb("expert_rows", [P, 14], I32)

    m.slot_x = [m.work[:, 256 * j:256 * (j + 1)] for j in range(GN)]
    m.slot_xt = [m.work[:, 1280 + 256 * j:1280 + 256 * (j + 1)].rearrange("p (k n) -> p k n", k=2) for j in range(GN)]
    m.w_mat = m.work[:, 2560:3072].rearrange("p (k n) -> p k n", k=2)
    at = [0]

    def view(*shape):
        n = 1
        for d in shape:
            n *= d
        v = m.work[:, at[0]:at[0] + n]
        at[0] += n
        if len(shape) == 2:
            v = v.rearrange("p (a b) -> p a b", a=shape[0])
        return v

    RW = D + 2 * HEADS
    m.rows = [view(ET, RW) for _ in range(3)]
    m.hot = [view(ET, P) for _ in range(3)]
    m.pen = [view(ET, P) for _ in range(2)]
    m.hott = [view(ET, P) for _ in range(2)]
    m.best = view(HEADS, P)
    m.msg = [view(ET * (D + HEADS)) for _ in range(2)]
    m.stage = [view(ET, 3) for _ in range(3)]
    m.stage_idx = [view(ET).bitcast(I32) for _ in range(3)]
    m.adm = [view(2 * HEADS) for _ in range(2)]
    m.drop = [view(HEADS) for _ in range(2)]
    m.fac = [view(HEADS) for _ in range(2)]
    m.score = [view(ET * HEADS) for _ in range(2)]
    m.wexp = [view(ET * HEADS) for _ in range(2)]
    assert at[0] <= 15000
    at[0] = 4 * GN * P
    m.w1 = [view(2, F) for _ in range(2)]
    m.w2 = [view(4, D) for _ in range(2)]
    m.b1 = [view(4) for _ in range(2)]
    m.b2 = [view(D) for _ in range(2)]
    assert at[0] <= 12000

    m.psum_all = ctx.enter_context(nc.psum_tensor("psum", [P, 8, 512], F32))
    m.psum = [m.psum_all[:, k, :] for k in range(8)]
    return m


SEMAPHORES = 40


class Stage:

    def __init__(self, nc, m):
        self.nc, self.m = nc, m
        if m.semaphores is None:
            m.semaphores = max(nc.free_semaphores) + 1 - 2 * SEMAPHORES

    def __enter__(self):
        nc, m = self.nc, self.m
        self.ctx = ExitStack()
        mine, other = m.semaphores + m.turn * SEMAPHORES, m.semaphores + (1 - m.turn) * SEMAPHORES
        numbers = iter(range(mine, mine + SEMAPHORES))
        m.sem = lambda name: self.ctx.enter_context(nc.semaphore(name, num=next(numbers)))
        self.block = nc.Block()
        block = self.block.__enter__()

        @block.sync
        def _(sp):
            sp.sem_clear(range(other, other + SEMAPHORES))

        m.turn = 1 - m.turn
        return block

    def __exit__(self, *error):
        self.block.__exit__(*error)
        return self.ctx.__exit__(*error)


def program(nc, a, y_out):
    with ExitStack() as ctx:
        m = memory(nc, ctx)
        table_sum = nc.dram_tensor("table_sum", [NT * P, D], F32).ap()
        table_gate = nc.dram_tensor("table_gate", [NT * P, 24], F32).ap()
        table_att = nc.dram_tensor("table_att", [NT * P, D + 2 * HEADS], F32).ap()
        sorted_dram = [[nc.dram_tensor(f"sorted{k}_{c}", [P * ET * n + P, 3], F32).ap() for c in range(COPIES)]
                       for k, n in enumerate((NCH, NCHG, NCH))]
        xn, hidden = m.xn[:, :, :], m.hidden

        with Stage(nc, m) as block:
            setup(nc, block, m, a["x"])
        graphs = ((a["src"], a["dst"], a["edge_weight"], NCH),
                  (a["L0_ffn_edge_index"][1], a["L0_ffn_edge_index"][0], None, NCHG),
                  (a["dst"], a["src"], None, NCH))
        for k, (key, val, w, nch) in enumerate(graphs):
            with Stage(nc, m) as block:
                sort_edges(nc, block, m, f"sort{k}", key, val, w, nch, sorted_dram[k], m.rec[k][:, :], m.bucket[k][:, :])

        with Stage(nc, m) as block:
            norm_rows(nc, block, m, "norm0", m.x[:, :, :], xn)
        with Stage(nc, m) as block:
            project(nc, block, m, "sup", a["L0_gnn_weight"], D, m.xn, table_sum)
        with Stage(nc, m) as block:
            sum_edges(nc, block, m, "sum", table_sum, m.rec[0], m.bucket[0], NCH)
        with Stage(nc, m) as block:
            add_sums(nc, block, m, "addsum", a["L0_gnn_bias"])
            norm_rows(nc, block, m, "norm1", m.x[:, :, :], xn)

        with Stage(nc, m) as block:
            project(nc, block, m, "gate", a["L0_ffn_W_gat"], 16, m.xn, table_gate, a["L0_ffn_att_src"], a["L0_ffn_att_dst"], keep_t=m.xt)
        with Stage(nc, m) as block:
            attend_edges(nc, block, m, "gatt", 16, table_gate, m.rec[1], m.bucket[1], NCHG)
        with Stage(nc, m) as block:
            gate_nodes(nc, block, m, "gates", a["L0_ffn_b_gat"], a["L0_ffn_ln_gamma"], a["L0_ffn_ln_beta"])
        with Stage(nc, m) as block:
            experts(nc, block, m, "ffn0", 4, m.x, (a["L0_ffn_W1"], a["L0_ffn_b1"], a["L0_ffn_W2"], a["L0_ffn_b2"]))

        with Stage(nc, m) as block:
            norm_rows(nc, block, m, "norm2", m.x[:, :, :], xn)
        layers = (("W1", "as1", "ad1", "b1"), ("W2", "as2", "ad2", "b2"), ("WN", "asN", "adN", "bN"))
        for k, (w, att_src, att_dst, b) in enumerate(layers):
            with Stage(nc, m) as block:
                project(nc, block, m, f"l{k}p", a["L1_gnn_" + w], D, m.xn if k == 0 else hidden, table_att,
                        a["L1_gnn_" + att_src], a["L1_gnn_" + att_dst])
            with Stage(nc, m) as block:
                attend_edges(nc, block, m, f"l{k}e", D, table_att, m.rec[2], m.bucket[2], NCH)
            with Stage(nc, m) as block:
                finish_layer(nc, block, m, f"l{k}f", k, a["L1_gnn_" + b])

        with Stage(nc, m) as block:
            norm_rows(nc, block, m, "norm3", m.x[:, :, :], xn)
        with Stage(nc, m) as block:
            turn_rows(nc, block, m, "turn")
            route(nc, block, m, "route", a["L1_ffn_Wr"], a["L1_ffn_br"], a["L1_ffn_W1"], a["L1_ffn_b1"], a["L1_ffn_W2"], a["L1_ffn_b2"])
        with Stage(nc, m) as block:
            experts(nc, block, m, "ffn1", 2, m.xn)
        with Stage(nc, m) as block:
            norm_rows(nc, block, m, "norm4", xn, xn)
        with Stage(nc, m) as block:
            finish(nc, block, m, a["L1_ffn_gamma"], a["L1_ffn_beta"], y_out)


_INS = ["x", "src", "dst", "edge_weight", "L0_gnn_weight", "L0_gnn_bias", "L0_ffn_W_gat", "L0_ffn_att_src", "L0_ffn_att_dst",
        "L0_ffn_b_gat", "L0_ffn_ln_gamma", "L0_ffn_ln_beta", "L0_ffn_W1", "L0_ffn_b1", "L0_ffn_W2", "L0_ffn_b2",
        "L0_ffn_edge_index", "L1_gnn_W1", "L1_gnn_as1", "L1_gnn_ad1", "L1_gnn_b1", "L1_gnn_W2", "L1_gnn_as2", "L1_gnn_ad2",
        "L1_gnn_b2", "L1_gnn_WN", "L1_gnn_asN", "L1_gnn_adN", "L1_gnn_bN", "L1_ffn_Wr", "L1_ffn_br", "L1_ffn_W1", "L1_ffn_b1",
        "L1_ffn_W2", "L1_ffn_b2", "L1_ffn_gamma", "L1_ffn_beta"]


def kernel(**inputs):
    import numpy as _np
    import concourse.bacc as _bacc
    from concourse import mybir as _mybir
    from concourse.bass_utils import run_bass_kernel_spmd as _run

    nc = _bacc.Bacc("TRN2", target_bir_lowering=False, num_devices=1)
    arrays, args = {}, {}
    for name in _INS:
        arr = _np.ascontiguousarray(inputs[name])
        arrays[f"in_{name}_dram"] = arr
        args[name] = nc.dram_tensor(f"in_{name}_dram", arr.shape, _mybir.dt.from_np(arr.dtype), kind="ExternalInput").ap()
    y = nc.dram_tensor("out_0_dram", (N, D), F32, kind="ExternalOutput").ap()
    program(nc, args, y)
    r = _run(nc, [arrays], core_ids=[0])
    return r.results[0]["out_0_dram"]
```

```python
from contextlib import ExitStack

import concourse.bass as bass
from concourse import mybir

P = 128
N = 3125
D = 256
E = 50000
EG = 32768
NT = (N + P - 1) // P
LAST = N - (NT - 1) * P
ET = 4
CH = ET * P
F = 512
UNROLL = 4
WORK = 17200
COPIES = 8
GN = 5
HEADS = 4
LN_EPS = 1e-5
BIG = 1e30

ALU = mybir.AluOpType
ACT = mybir.ActivationFunctionType
AX = mybir.AxisListType
F32 = mybir.dt.float32
BF16 = mybir.dt.bfloat16
I32 = mybir.dt.int32


def chunks_for(edges):
    worst = (edges + NT * (CH - 1)) // CH
    return -(-worst // UNROLL) * UNROLL


NCH = chunks_for(E)
NCHG = chunks_for(EG)


class Chain:

    def __init__(self, eng, sem):
        self.eng, self.sem, self.n, self.base, self.i, self.per = eng, sem, 0, 0, None, 0

    def enter(self, i, per):
        self.i, self.per, self.base, self.n = i, per, self.base + self.n, 0

    def leave(self, trips):
        assert self.n == self.per, (self.n, self.per)
        self.i, self.base, self.n = None, self.base + self.per * trips, 0

    def next(self, ins):
        ins.then_inc(self.sem, 1)
        self.n += 1
        at = self.base + self.n
        self.eng.wait_ge(self.sem, at if self.i is None else self.i * self.per + at)



def setup(nc, block, m, x_in):
    made, loaded, zeroed, iotas = m.sem("const_made"), m.sem("x_loaded"), m.sem("x_zeroed"), m.sem("iota_made")
    steps = m.sem("setup_steps")

    @block.gpsimd
    def _(pool):
        nc.gpsimd.memset(m.ident[:, :], 0.0).then_inc(made, 1)
        nc.gpsimd.memset(m.before[:, :], 1.0).then_inc(made, 1)
        nc.gpsimd.iota(m.iota_i[:, :], pattern=[[1, P]], base=0, channel_multiplier=0).then_inc(iotas, 1)
        nc.gpsimd.iota(m.iota_c[:, :], pattern=[[1, NCH]], base=0, channel_multiplier=0).then_inc(iotas, 1)
        nc.gpsimd.iota(m.pid_i[:, :], pattern=[[1, 2]], base=0, channel_multiplier=1).then_inc(iotas, 1)
        pool.wait_ge(made, 2)
        nc.gpsimd.affine_select(out=m.ident[:, :], in_=m.ident[:, :], compare_op=ALU.not_equal, fill=1.0, base=0,
                                pattern=[[-1, P]], channel_multiplier=1).then_inc(made, 1)
        nc.gpsimd.affine_select(out=m.before[:, :], in_=m.before[:, :], compare_op=ALU.is_gt, fill=0.0, base=0,
                                pattern=[[1, P]], channel_multiplier=-1).then_inc(made, 1)
        pool.wait_ge(made, 4)

    @block.vector
    def _(dve):
        nc.vector.memset(m.x[:, NT - 1, :], 0.0).then_inc(zeroed, 1)
        nc.vector.memset(m.ones[:, :], 1.0)
        dve.wait_ge(iotas, 3)
        nc.vector.tensor_copy(m.iota[:, :], m.iota_i[:, :])
        nc.vector.tensor_copy(m.iotac[:, :], m.iota_c[:, :])
        nc.vector.tensor_copy(m.pid[:, :], m.pid_i[:, :]).then_inc(steps, 1)
        dve.wait_ge(steps, 1)
        nc.vector.tensor_scalar(m.dummy[:, 0:1], m.pid[:, 0:1], float(P * ET * NCH), None, ALU.add)
        nc.vector.tensor_scalar(m.dummy[:, 1:2], m.pid[:, 0:1], float(P * ET * NCHG), None, ALU.add)
        nc.vector.tensor_tensor(m.lower[:, :, :], m.iota[:, 0:8].unsqueeze(1).to_broadcast([P, 8, 8]),
                                m.iota[:, 0:8].unsqueeze(2).to_broadcast([P, 8, 8]), ALU.is_lt).then_inc(steps, 1)
        dve.wait_ge(steps, 2)

    @block.sync
    def _(sp):
        sp.dma_start(m.x[:, 0:NT - 1, :], x_in[0:(NT - 1) * P, :].rearrange("(t p) d -> p t d", p=P)).then_inc(loaded, 16)
        sp.wait_ge(zeroed, 1)
        sp.dma_start(m.x[0:LAST, NT - 1, :], x_in[(NT - 1) * P:N, :]).then_inc(loaded, 16)
        sp.wait_ge(loaded, 32)




def columns_for(edges):
    return 400 if edges == E else 256


def place_edges(nc, block, m, name, key_in, val_in, w_in, nch, rec_dram, record, row, bucket, trip_count):
    edges = key_in.shape[0]
    fc = columns_for(edges)
    pf = edges // fc
    assert pf * fc == edges and fc % COPIES == 0
    ncol = nch * ET
    dummy = P * ncol

    loaded, cleared, rec_filled = (m.sem(f"{name}_{s}") for s in ("loaded", "cleared", "recfilled"))
    steps, ends, sums, placed = (m.sem(f"{name}_{s}") for s in ("steps", "ends", "sums", "placed"))
    key, hi, val = m.sort_key[:, 0:fc], m.sort_hi[:, 0:fc], m.sort_val[:, 0:fc]
    w, lo_i, place = m.sort_w[:, 0:fc], m.sort_lo[:, 0:fc], m.sort_place[:, 0:fc]
    mask = m.work[:, 10000:15000].bitcast(BF16)[:, 0:NT * fc].rearrange("p (b f) -> p b f", b=NT)
    count = m.work[:, 0:NT * fc].rearrange("p (b f) -> p b f", b=NT)
    small = m.sort_small
    cum, prev, own = small[:, 0, 0:NT], small[:, 1, :], small[:, 2, 0:NT]
    total, nchunk, cend, add = small[:, 3, 0:NT], small[:, 4, 0:NT], small[:, 5, 0:NT], small[:, 6, 0:NT]
    total_i = m.sort_small_i[:, :]
    ps_before, ps_total = m.psum[0][:, 0:NT], m.psum[0][:, 64:64 + NT]

    @block.sync
    def _(sp):
        sp.wait_ge(cleared, 1)
        sp.dma_start(key[0:pf, :], key_in.rearrange("(p f) -> p f", f=fc)).then_inc(loaded, 16)
        sp.dma_start(val[0:pf, :], val_in.rearrange("(p f) -> p f", f=fc)).then_inc(loaded, 16)
        if w_in is not None:
            sp.dma_start(w[0:pf, :], w_in.rearrange("(p f) -> p f", f=fc)).then_inc(loaded, 16)
        for k in range(COPIES):
            sp.dma_start(rec_dram[k][0:dummy, :].rearrange("(p c) k -> p (c k)", p=P), m.work[:, 0:3 * ncol]).then_inc(rec_filled, 16)

    @block.tensor
    def _(pe):
        pe.wait_ge(ends, 1)
        nc.tensor.matmul(ps_before, m.before[:, :], own, start=True, stop=True)
        nc.tensor.matmul(ps_total, m.ones[:, :], own, start=True, stop=True).then_inc(sums, 1)

    @block.vector
    def _(dve):
        chain = Chain(dve, steps)
        nc.vector.memset(key, NT * P)
        nc.vector.memset(val, 0)
        nc.vector.memset(w, 0.0)
        nc.vector.memset(prev, 0.0)
        nc.vector.memset(m.work[:, 0:3 * ncol], 0.0).then_inc(cleared, 1)
        dve.wait_ge(cleared, 1)
        dve.wait_ge(loaded, 48 if w_in is not None else 32)
        nc.vector.tensor_scalar(lo_i, key, P - 1, None, ALU.bitwise_and)
        chain.next(nc.vector.tensor_scalar(place, key, 7, None, ALU.logical_shift_right))
        chain.next(nc.vector.tensor_copy(hi, place))
        chain.next(nc.vector.tensor_tensor(mask, hi.unsqueeze(1).to_broadcast([P, NT, fc]),
                                           m.iota[:, 0:NT].unsqueeze(2).to_broadcast([P, NT, fc]), ALU.is_equal))
        dve.wait_ge(rec_filled, 16 * COPIES)
        flat = m.work[:, 10000:15000].bitcast(BF16)[:, 0:NT * fc]
        chain.next(nc.vector.tensor_tensor_scan(m.work[:, 0:NT * fc], m.ones[:, 0:1].to_broadcast([P, NT * fc]), flat,
                                                0.0, ALU.mult, ALU.add))
        chain.next(nc.vector.tensor_copy(cum, count[:, :, fc - 1]))
        nc.vector.tensor_copy(prev[:, 1:NT], cum[:, 0:NT - 1]).then_inc(placed, 1)
        dve.wait_ge(placed, 1)
        nc.vector.tensor_tensor(own, cum, prev[:, 0:NT], ALU.subtract).then_inc(ends, 1)
        dve.wait_ge(sums, 1)
        chain.next(nc.vector.tensor_scalar(total, ps_total, float(CH - 1), None, ALU.add))
        chain.next(nc.vector.tensor_copy(total_i, total))
        chain.next(nc.vector.tensor_scalar(total_i, total_i, 9, None, ALU.logical_shift_right))
        chain.next(nc.vector.tensor_copy(nchunk, total_i))
        chain.next(nc.vector.tensor_tensor_scan(cend, m.ones[:, 0:NT], nchunk, 0.0, ALU.mult, ALU.add))
        chain.next(nc.vector.tensor_tensor(add, cend, nchunk, ALU.subtract))
        chain.next(nc.vector.scalar_tensor_tensor(add, add, float(CH), ps_before, ALU.mult, ALU.add))
        chain.next(nc.vector.tensor_tensor(add, add, prev[:, 0:NT], ALU.subtract))
        chain.next(nc.vector.tensor_scalar(add, add, -1.0, None, ALU.add))
        chain.next(nc.vector.tensor_tensor(count, count, add.unsqueeze(2).to_broadcast([P, NT, fc]), ALU.add))
        chain.next(nc.vector.tensor_tensor(count, count, mask, ALU.mult))
        chain.next(nc.vector.tensor_reduce(hi, count.rearrange("p b f -> p f b"), AX.X, ALU.add))
        chain.next(nc.vector.tensor_copy(place, hi))
        nc.vector.tensor_scalar(m.sort_hi2[:, 0:fc], key, float(NT * P), m.dummy[:, 0:1] if nch == NCH else m.dummy[:, 1:2], ALU.is_ge, ALU.mult)
        chain.next(nc.vector.tensor_scalar(row, place, P - 1, None, ALU.bitwise_and))
        chain.next(nc.vector.tensor_scalar(place, place, 7, None, ALU.logical_shift_right))
        chain.next(nc.vector.scalar_tensor_tensor(hi, row, float(ncol), place, ALU.mult, ALU.add))
        chain.next(nc.vector.tensor_tensor(row, hi, m.sort_hi2[:, 0:fc], ALU.add))
        cmp = m.work[:, 0:NT * nch].rearrange("p (c b) -> p c b", b=NT)
        chain.next(nc.vector.tensor_tensor(cmp, cend.unsqueeze(1).to_broadcast([P, nch, NT]),
                                           m.iotac[:, 0:nch].unsqueeze(2).to_broadcast([P, nch, NT]), ALU.is_le))
        chain.next(nc.vector.tensor_reduce(m.sort_hi2[:, 0:nch], cmp, AX.X, ALU.add))
        chain.next(nc.vector.tensor_copy(bucket[:, 0:nch], m.sort_hi2[:, 0:nch]))
        nc.vector.tensor_scalar(record[:, :, 0], lo_i, 1.0, None, ALU.add)
        nc.vector.tensor_copy(record[:, :, 1], val)
        nc.vector.tensor_copy(record[:, :, 2], w)
        last = cend[:, NT - 1:NT]
        chain.next(nc.vector.tensor_scalar(hi[:, 0:nch // UNROLL], m.iotac[:, 0:nch // UNROLL], float(UNROLL), last, ALU.mult, ALU.is_lt))
        chain.next(nc.vector.tensor_reduce(m.sort_small[:, 7, 0:1], hi[:, 0:nch // UNROLL], AX.X, ALU.add))
        chain.next(nc.vector.tensor_scalar(trip_count, m.sort_small[:, 7, 0:1], -2.0, None, ALU.add))

def scatter_edges(nc, block, m, name, edges, rec_dram, record, row):
    half = COPIES // 2
    trips = columns_for(edges) // COPIES
    passed, staged = m.sem(f"{name}_passed"), m.sem(f"{name}_staged")
    sent = [m.dma_sem(f"{name}_sent{s}") for s in range(2)]

    @block.gpsimd
    def _(pool):
        def send(at, s, turn):
            nc.gpsimd.tensor_copy(m.stage_rec[s][:, :, :], record[:, bass.ds(at, half), :]).then_inc(staged, 1)
            nc.gpsimd.tensor_copy(m.stage_row[s][:, :], row[:, bass.ds(at, half)]).then_inc(staged, 1)
            pool.wait_ge(staged, turn * 2 + 2)
            pool.sem_inc(passed, 1)
            for f in range(half):
                nc.gpsimd.indirect_dma_start(
                    out=rec_dram[s * half + f], out_offset=bass.IndirectOffsetOnAxis(ap=m.stage_row[s][:, f:f + 1], axis=0),
                    in_=m.stage_rec[s][:, f, :], in_offset=None).then_inc(sent[s], 16)

        for s in range(2):
            send(half * s, s, s)
        with pool.Fori(1, trips) as i:
            for s in range(2):
                pool.wait_ge(sent[s], i * (half * 16))
                pool.sem_inc(passed, 1)
                send(i * COPIES + half * s, s, i * 2 + s)
        for s in range(2):
            pool.wait_ge(sent[s], trips * half * 16)


def merge_edges(nc, block, m, name, nch, rec_dram, rec):
    ncol = nch * ET
    steps, back = m.sem(f"{name}_steps"), m.sem(f"{name}_back")
    parts = m.work[:, 0:COPIES * 3 * ncol].rearrange("p (k c) -> p k c", k=COPIES)

    @block.sync
    def _(sp):
        for k in range(COPIES):
            sp.dma_start(parts[:, k, :], rec_dram[k][0:P * ncol, :].rearrange("(p c) k -> p (c k)", p=P)).then_inc(back, 16)

    @block.vector
    def _(dve):
        chain = Chain(dve, steps)
        dve.wait_ge(back, 16 * COPIES)
        for k in range(0, COPIES, 2):
            nc.vector.tensor_tensor(parts[:, k, :], parts[:, k, :], parts[:, k + 1, :], ALU.add)
        chain.next(nc.vector.tensor_copy(m.small[:, 0:1], m.ones[:, 0:1]))
        for k in range(0, COPIES, 4):
            chain.next(nc.vector.tensor_tensor(parts[:, k, :], parts[:, k, :], parts[:, k + 2, :], ALU.add))
        chain.next(nc.vector.tensor_tensor(rec, parts[:, 0, :], parts[:, 4, :], ALU.add))
        low = rec.rearrange("p (c k) -> p c k", k=3)[:, :, 0]
        chain.next(nc.vector.tensor_scalar(low, low, -1.0, None, ALU.add))



def norm_rows(nc, block, m, name, src, dst, square=None, done=None):
    tiles = NT
    steps, var_ready, std_ready = m.sem(f"{name}_steps"), m.sem(f"{name}_var"), m.sem(f"{name}_std")
    if square is None:
        square = m.work[:, 0:tiles * D].rearrange("p (t d) -> p t d", t=tiles)
    mean, var, std = (m.stats[:, k, 0:tiles] for k in range(3))

    def wide(a):
        return a.unsqueeze(2).to_broadcast([P, tiles, D])

    @block.vector
    def _(dve):
        chain = Chain(dve, steps)
        chain.next(nc.vector.tensor_reduce(mean, src, AX.X, ALU.add))
        chain.next(nc.vector.tensor_scalar(mean, mean, 1.0 / D, None, ALU.mult))
        chain.next(nc.vector.tensor_tensor(dst, src, wide(mean), ALU.subtract))
        chain.next(nc.vector.tensor_tensor(square, dst, dst, ALU.mult))
        chain.next(nc.vector.tensor_reduce(var, square, AX.X, ALU.add))
        nc.vector.tensor_scalar(var, var, 1.0 / D, LN_EPS, ALU.mult, ALU.add).then_inc(var_ready, 1)
        dve.wait_ge(std_ready, 1)
        chain.next(nc.vector.reciprocal(std, std))
        chain.next(nc.vector.tensor_tensor(dst, dst, wide(std), ALU.mult))
        if done is not None:
            dve.sem_inc(done, 1)

    @block.scalar
    def _(act):
        act.wait_ge(var_ready, 1)
        nc.scalar.activation(std, var, ACT.Sqrt).then_inc(std_ready, 1)



def project(nc, block, m, name, w_in, width, src, table, att_src=None, att_dst=None, keep_t=None, after=None):
    dh = width // HEADS
    rw = width + 2 * HEADS if att_src is not None else width
    staged, turned, turned_sb, done, taken, rows, stored, w_loaded, mult = (
        m.sem(f"{name}_{s}") for s in ("staged", "turned", "turnedsb", "done", "taken", "rows", "stored", "wloaded", "mult"))
    xs, xt = m.slot_x, m.slot_xt
    TB = 3
    ps_t = [m.psum[j % TB][:, 0:2 * P].rearrange("p (k n) -> p k n", k=2) for j in range(GN)]
    ps_h = [m.psum[TB + j][:, 0:width] for j in range(GN)]
    wt = m.w_mat[:, :, 0:width]
    acc = m.acc
    trips = NT // GN

    @block.sync
    def _(sp):
        if after is not None:
            sp.wait_ge(after, 1)
        sp.dma_start(wt, w_in.rearrange("(k p) n -> p k n", p=P)).then_inc(w_loaded, 16)
        if att_src is not None:
            sp.dma_start(m.att[:, 0, 0:width], att_src.rearrange("h c -> (h c)").partition_broadcast(P)).then_inc(w_loaded, 16)
            sp.dma_start(m.att[:, 1, 0:width], att_dst.rearrange("h c -> (h c)").partition_broadcast(P)).then_inc(w_loaded, 16)
        with sp.Fori(0, trips) as i:
            for j in range(GN):
                sp.wait_ge(taken if att_src is None else rows, i * GN + j + (2 if att_src is None else 1))
                sp.dma_start(table[bass.ds(i * (GN * P) + j * P, P), 0:rw], acc[:, i * GN + j, 0:rw]).then_inc(stored, 16)
        sp.wait_ge(stored, 16 * NT)

    @block.scalar
    def _(act):
        act.sem_inc(turned_sb, 1)
        if after is not None:
            act.wait_ge(after, 1)
        with act.Fori(0, trips) as i:
            for j in range(GN):
                act.wait_ge(turned, i * GN + 1)
                nc.scalar.copy(xs[j][:, :], src[:, i * GN + j, :]).then_inc(staged, 1)
            for j in range(GN):
                act.wait_ge(turned, i * GN + j + 2)
                act.wait_ge(done, i * GN + 1)
                nc.scalar.copy(xt[j][:, :, :], ps_t[j]).then_inc(turned_sb, 1)
                if keep_t is not None:
                    nc.scalar.copy(keep_t[:, :, bass.ds(i * (GN * P) + j * P, P)], ps_t[j]).then_inc(turned_sb, 1)

    per = 2 if keep_t is not None else 1

    @block.tensor
    def _(pe):
        pe.sem_inc(turned, 1)
        pe.sem_inc(done, 1)
        with pe.Fori(0, trips) as i:
            for j in range(GN):
                pe.wait_ge(staged, i * GN + j + 1)
                pe.wait_ge(turned_sb, i * (GN * per) + (max(0, j - TB + 1) * per + 1))
                for k in range(2):
                    ins = nc.tensor.transpose(ps_t[j][:, k, :], xs[j][:, k * P:(k + 1) * P], m.ident[:, :])
                ins.then_inc(turned, 1)
            for j in range(GN):
                pe.wait_ge(turned_sb, i * (GN * per) + ((j + 1) * per + 1))
                pe.wait_ge(w_loaded, 16 if att_src is None else 48)
                pe.wait_ge(taken, i * GN + 1)
                for k in range(2):
                    ins = nc.tensor.matmul(ps_h[j], xt[j][:, k, :], wt[:, k, :], start=k == 0, stop=k == 1)
                ins.then_inc(done, 1)

    @block.vector
    def _(dve):
        chain = Chain(dve, mult)
        dve.sem_inc(taken, 1)
        if att_src is not None:
            dve.wait_ge(w_loaded, 48)
        with dve.Fori(0, trips) as i:
            chain.enter(i, 0 if att_src is None else 2 * GN)
            for j in range(GN):
                t = i * GN + j
                dve.wait_ge(done, i * GN + j + 2)
                if att_src is None:
                    nc.vector.tensor_scalar(acc[:, t, 0:width], ps_h[j], 0.0, None, ALU.add).then_inc(taken, 1)
                    continue
                heads = acc[:, t, 0:width + HEADS].rearrange("p (h w) -> p h w", h=HEADS)
                prod, sm = m.prod, m.small
                nc.vector.tensor_scalar(heads[:, :, 0:dh], ps_h[j].rearrange("p (h c) -> p h c", h=HEADS), 0.0, None, ALU.add)
                nc.vector.tensor_scalar(heads[:, :, dh], m.ones[:, 0:HEADS], 1.0, None, ALU.mult)
                nc.vector.tensor_tensor(prod[:, 1, 0:width], ps_h[j], m.att[:, 1, 0:width], ALU.mult)
                nc.vector.tensor_tensor(prod[:, 0, 0:width], ps_h[j], m.att[:, 0, 0:width], ALU.mult).then_inc(taken, 1)
                dve.wait_ge(taken, t + 2)
                nc.vector.tensor_reduce(acc[:, t, rw + HEADS:rw + 2 * HEADS], prod[:, 1, 0:width].rearrange("p (h c) -> p h c", h=HEADS), AX.X, ALU.add)
                nc.vector.tensor_reduce(acc[:, t, width + HEADS:rw], prod[:, 0, 0:width].rearrange("p (h c) -> p h c", h=HEADS),
                                        AX.X, ALU.add).then_inc(rows, 1)
                dve.wait_ge(rows, t + 1)
                chain.next(nc.vector.tensor_tensor(sm[:, 0:HEADS], acc[:, t, rw + HEADS:rw + 2 * HEADS], acc[:, t, width + HEADS:rw], ALU.add))
                chain.next(nc.vector.scalar_tensor_tensor(acc[:, t, rw:rw + HEADS], sm[:, 0:HEADS], 0.2, sm[:, 0:HEADS],
                                                          ALU.mult, ALU.max))
        chain.leave(trips)



def trip_bounds(nch):
    edges = E if nch == NCH else EG
    return -(-edges // (CH * UNROLL)) - 2, nch // UNROLL - 2


def sum_edges(nc, block, m, name, table, rec, bucket, trip_count, nch):
    passed, copied, staged, hot, summed, taken, out = (m.sem(f"{name}_{s}") for s in ("passed", "copied", "staged", "hot", "summed", "taken", "out"))
    landed = [m.dma_sem(f"{name}_landed{s}") for s in range(UNROLL)]
    rows = [m.rows[s][:, :, 0:D] for s in range(UNROLL)]
    ps = [m.psum[s][:, 0:D] for s in range(UNROLL)]
    nrec = ET * 3
    least, most = trip_bounds(nch)

    @block.vector
    def _(dve):
        def stage(c, s):
            nc.vector.tensor_scalar(m.stage[s][:, :, :].rearrange("p t k -> p (t k)"), rec[:, bass.ds(c * nrec, nrec)], 0.0, None, ALU.add).then_inc(copied, 1)
            dve.wait_ge(copied, c + 1)
            nc.vector.tensor_copy(m.stage_idx[s][:, :], m.stage[s][:, :, 1]).then_inc(staged, 1)
            for t in range(ET):
                ins = nc.vector.tensor_scalar(m.hot[s][:, t, :], m.iota[:, :], m.stage[s][:, t, 0:1], m.stage[s][:, t, 2:3],
                                              ALU.is_equal, ALU.mult)
            ins.then_inc(hot, 1)

        def take(c, s):
            b = dve.value_load(bucket[0:1, bass.ds(c, 1)], min_val=0, max_val=NT)
            dve.wait_ge(summed, c + 1)
            dve.wait_ge(taken, c + 1)
            nc.vector.tensor_tensor(m.acc[:, b, 0:D], m.acc[:, b, 0:D], ps[s], ALU.add).then_inc(taken, 1)

        dve.sem_inc(taken, 1)
        nc.vector.memset(m.acc[:, :, :], 0.0).then_inc(out, 1)
        dve.wait_ge(out, 1)
        for s in range(UNROLL):
            stage(s, s)
        trips = dve.value_load(trip_count, min_val=least, max_val=most)
        with dve.Fori(0, trips + 1) as i:
            for s in range(UNROLL):
                take(i * UNROLL + s, s)
                stage(i * UNROLL + (UNROLL + s), s)
        for s in range(UNROLL):
            take(trips * UNROLL + (UNROLL + s), s)

    @block.gpsimd
    def _(pool):
        trips = pool.value_load(trip_count, min_val=least, max_val=most)
        with pool.Fori(0, trips + 2) as i:
            for s in range(UNROLL):
                pool.wait_ge(staged, i * UNROLL + s + 1)
                pool.sem_inc(passed, 1)
                for t in range(ET):
                    nc.gpsimd.indirect_dma_start(
                        out=rows[s][:, t, :], out_offset=None, in_=table,
                        in_offset=bass.IndirectOffsetOnAxis(ap=m.stage_idx[s][:, t:t + 1], axis=0)).then_inc(landed[s], 16)

    @block.tensor
    def _(pe):
        trips = pe.value_load(trip_count, min_val=least, max_val=most)
        with pe.Fori(0, trips + 2) as i:
            for s in range(UNROLL):
                pe.wait_ge(hot, i * UNROLL + s + 1)
                pe.wait_ge(landed[s], i * (16 * ET) + 16 * ET)
                for t in range(ET):
                    ins = nc.tensor.matmul(ps[s], m.hot[s][:, t, :], rows[s][:, t, :], start=t == 0, stop=t == ET - 1)
                ins.then_inc(summed, 1)


def attend_edges(nc, block, m, name, width, table, rec, bucket, trip_count, nch):
    dh = width // HEADS
    w1 = dh + 1
    hw = HEADS * w1
    rw = hw + HEADS
    nrec = ET * 3
    SL = 4
    s_ = lambda n: m.sem(f"{name}_{n}")
    passed, copied, staged, hot, pen_r, offered, halved, hott, hott_sb, best, best_t, top, spread, score, wexp, shrink, scaled, summed, taken, kept, chain_s = (
        s_(n) for n in ("passed", "copied", "staged", "hot", "pen", "offered", "halved", "hott", "hottsb", "best", "bestt", "top", "spread", "score", "wexp",
                        "shrink", "scaled", "summed", "taken", "kept", "chain"))
    landed = [m.dma_sem(f"{name}_landed{s}") for s in range(SL)]
    rows = [m.rows[s][:, :, 0:rw] for s in range(SL)]
    ps_hott, ps_best, ps_spread = m.psum[0], m.psum[1], m.psum[2]
    ps_sum = [m.psum[3 + s][:, 0:hw] for s in range(2)]
    least, most = trip_bounds(nch)
    U = UNROLL

    @block.gpsimd
    def _(pool):
        def gather(c, s):
            pool.wait_ge(staged, c + 1)
            pool.sem_inc(passed, 1)
            if not isinstance(c, int) or c >= SL:
                pool.wait_ge(scaled, c + (1 - SL))
                pool.sem_inc(passed, 1)
            for t in range(ET):
                nc.gpsimd.indirect_dma_start(
                    out=rows[s][:, t, :], out_offset=None, in_=table,
                    in_offset=bass.IndirectOffsetOnAxis(ap=m.stage_idx[s][:, t:t + 1], axis=0)).then_inc(landed[s], 16)

        def scale(c, s, z):
            if not isinstance(c, int) or c >= 2:
                pool.wait_ge(summed, c + (-1))
                pool.sem_inc(passed, 1)
            pool.wait_ge(wexp, c + 1)
            pool.sem_inc(passed, 1)
            nc.gpsimd.tensor_tensor(
                m.msg[z][:, 0:ET * hw].rearrange("p (t h w) -> p t h w", t=ET, h=HEADS),
                rows[s][:, :, 0:hw].rearrange("p t (h w) -> p t h w", h=HEADS),
                m.wexp[z][:, :].rearrange("p (t h) -> p t h", t=ET).unsqueeze(3).to_broadcast([P, ET, HEADS, w1]),
                ALU.mult).then_inc(scaled, 1)

        def body(c, s):
            gather(c, s)
            if not isinstance(c, int) or c >= 3:
                scale(c + (-3), (s + 1) % SL, (s + 1) % 2)

        trips = pool.value_load(trip_count, min_val=least, max_val=most)
        for c in range(SL):
            body(c, c)
        with pool.Fori(0, trips + 1) as i:
            for s in range(SL):
                body(i * SL + (SL + s), s)
        for s in range(1, SL):
            scale(trips * SL + (SL + s), s, s % 2)

    @block.vector
    def _(dve):
        chain = Chain(dve, chain_s)

        def copy_records(c, s):
            nc.vector.tensor_scalar(m.stage[s][:, :, :].rearrange("p t k -> p (t k)"), rec[:, bass.ds(c * nrec, nrec)], 0.0, None, ALU.add).then_inc(copied, 1)

        def copy_index(c, s):
            dve.wait_ge(copied, c + 1)
            nc.vector.tensor_copy(m.stage_idx[s][:, :], m.stage[s][:, :, 1]).then_inc(staged, 1)

        def one_hot(c, s):
            nc.vector.tensor_tensor(m.hot[s][:, :, :], m.iota[:, :].unsqueeze(1).to_broadcast([P, ET, P]),
                                    m.stage[s][:, :, 0:1].to_broadcast([P, ET, P]), ALU.is_equal).then_inc(hot, 1)

        def halve(c, z):
            offer = m.offer[z]
            dve.wait_ge(offered, c + 1)
            nc.vector.tensor_tensor(offer[:, 0:2, :], offer[:, 0:2, :], offer[:, 2:4, :], ALU.max).then_inc(halved, 1)

        def pick_best(c, z):
            dve.wait_ge(halved, c + 1)
            nc.vector.tensor_tensor(m.best[:, :], m.offer[z][:, 0, :], m.offer[z][:, 1, :], ALU.max).then_inc(best, 1)

        def load_bucket(c):
            return dve.value_load(bucket[0:1, bass.ds(c, 1)], min_val=0, max_val=NT)

        def raise_top(b, c, z, stage=None):
            adm, drop, sm, old = m.adm[z], m.drop[z], m.small, m.old
            if not isinstance(c, int) or c:
                dve.wait_ge(kept, c)
            nc.vector.tensor_scalar(old[:, :], m.acc[:, b, hw:hw + 3 * HEADS], 0.0, None, ALU.add)
            dve.wait_ge(best_t, c + 1)
            chain.next(nc.vector.tensor_reduce(sm[:, 0:4], ps_best[:, :].rearrange("p (h e) -> p h e", h=HEADS), AX.X, ALU.max))
            if stage:
                copy_records(*stage)
            chain.next(nc.vector.tensor_tensor(adm[:, 0:4], old[:, 0:4], sm[:, 0:4], ALU.max))
            nc.vector.tensor_copy(adm[:, 8:12], old[:, 8:12])
            if stage:
                copy_index(*stage)
            chain.next(nc.vector.tensor_tensor(sm[:, 4:8], adm[:, 0:4], old[:, 8:12], ALU.add))
            chain.next(nc.vector.scalar_tensor_tensor(adm[:, 4:8], sm[:, 4:8], 0.2, sm[:, 4:8], ALU.mult, ALU.max))
            nc.vector.tensor_tensor(drop[:, :], old[:, 4:8], adm[:, 4:8], ALU.subtract).then_inc(top, 1)
            dve.wait_ge(top, c + 1)
            nc.vector.tensor_scalar(m.acc[:, b, hw:hw + 2 * HEADS], adm[:, 0:8], 0.0, None, ALU.add).then_inc(kept, 1)

        def scores(c, s, z):
            sc = m.score[z]
            dve.wait_ge(spread, c + 1)
            sp = ps_spread[:, 0:8 * ET].rearrange("p (t k) -> p t k", t=ET)
            v = sc[:, :].rearrange("p (t h) -> p t h", t=ET)
            chain.next(nc.vector.tensor_tensor(v, rows[s][:, :, hw:rw], sp[:, :, 4:8], ALU.add))
            chain.next(nc.vector.scalar_tensor_tensor(sc[:, :], sc[:, :], 0.2, sc[:, :], ALU.mult, ALU.max))
            chain.next(nc.vector.tensor_tensor(v, v, sp[:, :, 0:4], ALU.subtract))
            nc.vector.tensor_scalar(sc[:, :], sc[:, :], 0.0, None, ALU.min).then_inc(score, 1)

        def take(b, c, z):
            acc = m.acc[:, b, 0:hw]
            dve.wait_ge(shrink, c + 1)
            if not isinstance(c, int) or c:
                dve.wait_ge(taken, c)
            chain.next(nc.vector.tensor_tensor(acc.rearrange("p (h w) -> p h w", h=HEADS), acc.rearrange("p (h w) -> p h w", h=HEADS),
                                               m.fac[z][:, :].unsqueeze(2).to_broadcast([P, HEADS, w1]), ALU.mult))
            dve.wait_ge(summed, c + 1)
            nc.vector.tensor_tensor(acc, acc, ps_sum[z], ALU.add).then_inc(taken, 1)

        def body(c, k, b, b_before, left=U):
            s, z = k % SL, k % 2
            raise_top(b, c, z, (c + 3, (s + 3) % SL) if left >= 3 else None)
            if left >= 2:
                one_hot(c + 2, (s + 2) % SL)
            if left >= 1:
                halve(c + 1, 1 - z)
            b_next = load_bucket(c + 1) if k < U - 1 else None
            scores(c, s, z)
            if left >= 1:
                pick_best(c + 1, 1 - z)
            if b_before is not None:
                take(b_before, c + (-1), 1 - z)
            return b_next

        def bodies(c, b_before, left=2 * U):
            b = load_bucket(c)
            for k in range(U):
                b, b_before = body(c + k, k, b, b_before, left - 1 - k), b
            return b_before

        chain.next(nc.vector.memset(m.acc[:, NT, :], 0.0))
        trips = dve.value_load(trip_count, min_val=least, max_val=most)
        for c in range(3):
            copy_records(c, c)
            copy_index(c, c)
        for c in range(2):
            one_hot(c, c)
        halve(0, 0)
        pick_best(0, 0)
        bodies(0, None)
        per = 4 + 3 + 1
        with dve.Fori(0, trips) as i:
            chain.enter(i, U * per)
            bodies(i * U + U, load_bucket(i * U + (U - 1)))
        chain.leave(trips)
        last = bodies(trips * U + U, load_bucket(trips * U + (U - 1)), U)
        take(last, trips * U + (2 * U - 1), (U - 1) % 2)

    @block.scalar
    def _(act):
        def fence(c, s):
            act.wait_ge(hot, c + 1)
            if not isinstance(c, int) or c:
                act.wait_ge(offered, c)
            nc.scalar.activation(m.pen[:, :, :], m.hot[s][:, :, :], ACT.Copy, bias=-BIG, scale=BIG).then_inc(pen_r, 1)

        def copy_turned(c, s):
            act.wait_ge(hott, c + 1)
            nc.scalar.copy(m.hott[s][:, :, :].rearrange("p t e -> p (t e)"), ps_hott[:, :]).then_inc(hott_sb, 1)

        pairs = [(t, h) for t in range(ET) for h in range(HEADS)]

        def offer(c, s, i, z, first=0, last=len(pairs)):
            if first == 0:
                act.wait_ge(landed[s], i * (16 * ET) + 16 * ET)
                act.wait_ge(pen_r, c + 1)
                if not isinstance(c, int) or c >= 2:
                    act.wait_ge(best, c + (-1))
            for t, h in pairs[first:last]:
                ins = nc.scalar.activation(m.offer[z][:, t, h * P:(h + 1) * P], m.pen[:, t, :], ACT.Identity,
                                           bias=rows[s][:, t, hw + h:hw + h + 1])
            if last == len(pairs):
                ins.then_inc(offered, 1)

        def back(c, k, i, left=U):
            z, s2, i2 = k % 2, (k + 2) % SL, i + (k + 2) // SL
            act.wait_ge(top, c + 1)
            nc.scalar.activation(m.fac[z][:, :], m.drop[z][:, :], ACT.Exp).then_inc(shrink, 1)
            if left >= 1:
                copy_turned(c + 1, (k + 1) % SL)
            if left >= 2:
                fence(c + 2, s2)
                offer(c + 2, s2, i2, z, last=early)
            act.wait_ge(score, c + 1)
            nc.scalar.activation(m.wexp[z][:, :], m.score[z][:, :], ACT.Exp).then_inc(wexp, 1)
            if left >= 2:
                offer(c + 2, s2, i2, z, first=early)

        early = 5
        trips = act.value_load(trip_count, min_val=least, max_val=most)
        for c in range(2):
            fence(c, c)
            offer(c, c, 0, c)
            if c == 0:
                copy_turned(0, 0)
        for k in range(U):
            back(k, k, 0)
        with act.Fori(0, trips) as i:
            for k in range(U):
                back(i * U + (U + k), k, i + 1)
        for k in range(U):
            back(trips * U + (U + k), k, trips + 1, left=U - 1 - k)

    @block.tensor
    def _(pe):
        def turn_hot(c, s):
            pe.wait_ge(hot, c + 1)
            pe.wait_ge(hott_sb, c)
            for t in range(ET):
                ins = nc.tensor.transpose(ps_hott[:, t * P:(t + 1) * P], m.hot[s][:, t, :], m.ident[:, :])
            ins.then_inc(hott, 1)

        def turn_best(c):
            pe.wait_ge(best, c + 1)
            pe.wait_ge(top, c)
            for h in range(HEADS):
                ins = nc.tensor.transpose(ps_best[:, h * P:(h + 1) * P], m.best[:, h * P:(h + 1) * P], m.ident[:, :])
            ins.then_inc(best_t, 1)

        def spread_top(c, s, z):
            pe.wait_ge(top, c + 1)
            pe.wait_ge(hott_sb, c + 1)
            for t in range(ET):
                ins = nc.tensor.matmul(ps_spread[:, 8 * t:8 * t + 8], m.hott[s][:, t, :], m.adm[z][:, 4:12], start=True, stop=True)
            ins.then_inc(spread, 1)

        def sums(c, s, z, tiles):
            if tiles[0] == 0:
                pe.wait_ge(scaled, c + 1)
                if not isinstance(c, int) or c >= 2:
                    pe.wait_ge(taken, c + (-1))
            for t in tiles:
                ins = nc.tensor.matmul(ps_sum[z], m.hot[s][:, t, :], m.msg[z][:, t * hw:(t + 1) * hw], start=t == 0, stop=t == ET - 1)
            if tiles[-1] == ET - 1:
                ins.then_inc(summed, 1)

        def body(c, k, first=False, left=U):
            s, z = k % SL, k % 2
            if not first:
                sums(c + (-1), (s + 3) % SL, 1 - z, range(1))
            spread_top(c, s, z)
            if not first:
                sums(c + (-1), (s + 3) % SL, 1 - z, range(1, ET))
            if left >= 1:
                turn_best(c + 1)
            if left >= 2:
                turn_hot(c + 2, (s + 2) % SL)

        trips = pe.value_load(trip_count, min_val=least, max_val=most)
        turn_hot(0, 0)
        turn_best(0)
        turn_hot(1, 1)
        for k in range(U):
            body(k, k, first=k == 0)
        with pe.Fori(0, trips) as i:
            for k in range(U):
                body(i * U + (U + k), k)
        for k in range(U):
            body(trips * U + (U + k), k, left=U - 1 - k)
        sums(trips * U + (2 * U - 1), U - 1, (U - 1) % 2, range(ET))



def add_sums(nc, block, m, name, bias_in):
    loaded, steps = m.sem(f"{name}_loaded"), m.sem(f"{name}_steps")

    @block.sync
    def _(sp):
        sp.dma_start(m.bias[:, :], bias_in.partition_broadcast(P)).then_inc(loaded, 16)

    @block.vector
    def _(dve):
        chain = Chain(dve, steps)
        chain.next(nc.vector.tensor_tensor(m.x[:, :, :], m.x[:, :, :], m.acc[:, 0:NT, 0:D], ALU.add))
        dve.wait_ge(loaded, 16)
        chain.next(nc.vector.tensor_tensor(m.x[:, :, :], m.x[:, :, :], m.bias[:, :].unsqueeze(1).to_broadcast([P, NT, D]), ALU.add))


def attended(nc, m, chain, width, out):
    dh = width // HEADS
    acc = m.acc[:, 0:NT, 0:width + HEADS].rearrange("p t (h w) -> p t h w", h=HEADS)
    den = m.den[:, :, :]
    chain.next(nc.vector.tensor_scalar(den, acc[:, :, :, dh], 1e-16, None, ALU.add))
    chain.next(nc.vector.reciprocal(den, den))
    chain.next(nc.vector.tensor_tensor(out.rearrange("p t (h c) -> p t h c", h=HEADS), acc[:, :, :, 0:dh],
                                       den.unsqueeze(3).to_broadcast([P, NT, HEADS, dh]), ALU.mult))


def finish_layer(nc, block, m, name, layer, bias_in):
    loaded, steps = m.sem(f"{name}_loaded"), m.sem(f"{name}_steps")
    xt = m.hidden

    @block.sync
    def _(sp):
        sp.dma_start(m.bias[:, :], bias_in.partition_broadcast(P)).then_inc(loaded, 16)

    @block.vector
    def _(dve):
        chain = Chain(dve, steps)
        attended(nc, m, chain, D, xt)
        dve.wait_ge(loaded, 16)
        chain.next(nc.vector.tensor_tensor(xt, xt, m.bias[:, :].unsqueeze(1).to_broadcast([P, NT, D]), ALU.add))
        if layer == 0:
            chain.next(nc.vector.scalar_tensor_tensor(xt, xt, 0.0, m.xn[:, :, :], ALU.max, ALU.add))
        elif layer == 1:
            chain.next(nc.vector.tensor_scalar(xt, xt, 0.0, None, ALU.max))
        else:
            chain.next(nc.vector.tensor_tensor(xt, xt, m.xn[:, :, :], ALU.add))
            chain.next(nc.vector.scalar_tensor_tensor(m.x[:, :, :], xt, 0.0, m.x[:, :, :], ALU.max, ALU.add))


def gate_nodes(nc, block, m, name, b_in, gamma_in, beta_in):
    NE = 4
    loaded, steps, var_ready, std_ready, to_exp, exped = (m.sem(f"{name}_{s}") for s in ("loaded", "steps", "var", "std", "toexp", "exped"))
    W = 16
    at = [0]

    def take(*shape):
        n = 1
        for d in shape:
            n *= d
        v = m.work[:, at[0]:at[0] + n]
        at[0] += n
        return v

    agg = take(NT * W).rearrange("p (t c) -> p t c", t=NT)
    sq = take(NT * W).rearrange("p (t c) -> p t c", t=NT)
    mean, var, std, top, tot = (take(NT) for _ in range(5))
    sc = take(NT * NE).rearrange("p (t e) -> p t e", t=NT)
    rank = take(NT * NE).rearrange("p (t e) -> p t e", t=NT)
    gt = take(NT * NE * NE).rearrange("p (t i j) -> p t i j", t=NT, i=NE)
    eq = take(NT * NE * NE).rearrange("p (t i j) -> p t i j", t=NT, i=NE)

    def wide(a, w=W):
        return a.unsqueeze(2).to_broadcast([P, NT, w])

    def par(k):
        return m.bias[:, k * W:(k + 1) * W].unsqueeze(1).to_broadcast([P, NT, W])

    @block.sync
    def _(sp):
        for k, a in enumerate((b_in, gamma_in, beta_in)):
            sp.dma_start(m.bias[:, k * W:(k + 1) * W], a.partition_broadcast(P)).then_inc(loaded, 16)

    @block.vector
    def _(dve):
        chain = Chain(dve, steps)
        attended(nc, m, chain, W, agg)
        dve.wait_ge(loaded, 48)
        chain.next(nc.vector.tensor_tensor(agg, agg, par(0), ALU.add))
        chain.next(nc.vector.tensor_reduce(mean, agg, AX.X, ALU.add))
        chain.next(nc.vector.tensor_scalar(mean, mean, 1.0 / W, None, ALU.mult))
        chain.next(nc.vector.tensor_tensor(agg, agg, wide(mean), ALU.subtract))
        chain.next(nc.vector.tensor_tensor(sq, agg, agg, ALU.mult))
        chain.next(nc.vector.tensor_reduce(var, sq, AX.X, ALU.add))
        nc.vector.tensor_scalar(var, var, 1.0 / W, LN_EPS, ALU.mult, ALU.add).then_inc(var_ready, 1)
        dve.wait_ge(std_ready, 1)
        chain.next(nc.vector.reciprocal(std, std))
        chain.next(nc.vector.tensor_tensor(agg, agg, wide(std), ALU.mult))
        chain.next(nc.vector.tensor_tensor(agg, agg, par(1), ALU.mult))
        chain.next(nc.vector.tensor_tensor(agg, agg, par(2), ALU.add))
        chain.next(nc.vector.tensor_reduce(sc, agg.rearrange("p t (h e) -> p t e h", h=HEADS), AX.X, ALU.add))
        chain.next(nc.vector.tensor_scalar(sc, sc, 1.0 / HEADS, None, ALU.mult))
        rank_of(nc, m, chain, sc, gt, eq, rank, NE, NT)
        chain.next(nc.vector.tensor_reduce(top, sc, AX.X, ALU.max))
        nc.vector.tensor_tensor(sc, sc, wide(top, NE), ALU.subtract).then_inc(to_exp, 1)
        chain.next(nc.vector.tensor_scalar(rank, rank, 2.0, None, ALU.is_lt))
        dve.wait_ge(exped, 1)
        chain.next(nc.vector.tensor_tensor(sc, sc, rank, ALU.mult))
        chain.next(nc.vector.tensor_reduce(tot, sc, AX.X, ALU.add))
        chain.next(nc.vector.reciprocal(tot, tot))
        chain.next(nc.vector.tensor_tensor(m.gates[:, :, :].rearrange("p e t -> p t e"), sc, wide(tot, NE), ALU.mult))

    @block.scalar
    def _(act):
        act.wait_ge(var_ready, 1)
        nc.scalar.activation(std, var, ACT.Sqrt).then_inc(std_ready, 1)
        act.wait_ge(to_exp, 1)
        nc.scalar.activation(sc, sc, ACT.Exp).then_inc(exped, 1)


def rank_of(nc, m, chain, sc, gt, eq, rank, ne, nt):
    at_j = sc.unsqueeze(2).to_broadcast([P, nt, ne, ne])
    at_i = sc.unsqueeze(3).to_broadcast([P, nt, ne, ne])
    chain.next(nc.vector.tensor_tensor(gt, at_j, at_i, ALU.is_gt))
    chain.next(nc.vector.tensor_tensor(eq, at_j, at_i, ALU.is_equal))
    chain.next(nc.vector.tensor_tensor(eq, eq, m.lower[:, 0:ne, 0:ne].unsqueeze(1).to_broadcast([P, nt, ne, ne]), ALU.mult))
    chain.next(nc.vector.tensor_tensor(gt, gt, eq, ALU.add))
    chain.next(nc.vector.tensor_reduce(rank, gt, AX.X, ALU.add))


def turn_rows(nc, block, m, name):
    staged, turned, out = m.sem(f"{name}_staged"), m.sem(f"{name}_turned"), m.sem(f"{name}_out")
    ps_t = [m.psum[j][:, 0:2 * P].rearrange("p (k n) -> p k n", k=2) for j in range(GN)]

    @block.scalar
    def _(act):
        act.sem_inc(out, 1)
        with act.Fori(0, NT // GN) as i:
            for j in range(GN):
                act.wait_ge(turned, i * GN + 1)
                nc.scalar.copy(m.slot_x[j][:, :], m.xn[:, i * GN + j, :]).then_inc(staged, 1)
            for j in range(GN):
                act.wait_ge(turned, i * GN + j + 2)
                nc.scalar.copy(m.xt[:, :, bass.ds(i * (GN * P) + j * P, P)], ps_t[j]).then_inc(out, 1)

    @block.tensor
    def _(pe):
        pe.sem_inc(turned, 1)
        with pe.Fori(0, NT // GN) as i:
            for j in range(GN):
                pe.wait_ge(staged, i * GN + j + 1)
                pe.wait_ge(out, i * GN + 1)
                for k in range(2):
                    ins = nc.tensor.transpose(ps_t[j][:, k, :], m.slot_x[j][:, k * P:(k + 1) * P], m.ident[:, :])
                ins.then_inc(turned, 1)


def route(nc, block, m, name, wr_in, br_in, w1_in, b1_in, w2_in, b2_in):
    NE = 8
    capacity = float(-(-int(N * 1.25) // NE))
    assert capacity == 489.0
    loaded, steps, summed, mean_in, logits_in, e1, e1d, e2, e2d, e3, e3d, index, wide_in = (
        m.sem(f"{name}_{s}") for s in ("loaded", "steps", "summed", "mean", "logits", "e1", "e1d", "e2", "e2d", "e3", "e3d",
                                       "index", "wide"))
    got = m.dma_sem(f"{name}_got")
    work = m.work
    colsum = work[:, 12000:12000 + D]
    mu = work[:, 12256:12258]
    muw = work[:, 12300:12300 + 2 * P].rearrange("p (k n) -> p k n", k=2)
    wr = work[:, 12600:12600 + 2 * NE].rearrange("p (k e) -> p k e", k=2)
    br = work[:, 12620:12620 + NE]
    rw, ex, scl = work[:, 12640:12648], work[:, 12650:12658], work[:, 12660:12668]
    top, tot = work[:, 12670:12671], work[:, 12671:12672]
    gt = work[:, 12700:12764].rearrange("p (t i j) -> p t i j", t=1, i=NE)
    eq = work[:, 12764:12828].rearrange("p (t i j) -> p t i j", t=1, i=NE)
    rank = work[:, 12830:12838]
    sel, val, num = work[:, 12840:12848], work[:, 12850:12852], work[:, 12852:12854]
    diff = work[:, 12854:12855]
    ps_mean, ps_logit = m.psum[6][:, 0:2], m.psum[7][:, 0:NE]
    offs = work[:, 12860:12874]
    offs_i = m.expert_rows

    @block.sync
    def _(sp):
        sp.dma_start(wr, wr_in.rearrange("(k p) e -> p k e", p=P)).then_inc(loaded, 16)
        sp.dma_start(br, br_in.partition_broadcast(P)).then_inc(loaded, 16)

    @block.tensor
    def _(pe):
        pe.wait_ge(summed, 1)
        for k in range(2):
            nc.tensor.matmul(ps_mean[:, k:k + 1], colsum[:, k * P:(k + 1) * P], m.ones[:, 0:1], start=True, stop=False)
            ins = nc.tensor.matmul(ps_mean[:, k:k + 1], m.xn[0:LAST, NT - 1, k * P:(k + 1) * P], m.ones[0:LAST, 0:1], start=False, stop=True)
        ins.then_inc(mean_in, 1)
        pe.wait_ge(wide_in, 1)
        pe.wait_ge(loaded, 32)
        for k in range(2):
            ins = nc.tensor.matmul(ps_logit, muw[:, k, :], wr[:, k, :], start=k == 0, stop=k == 1)
        ins.then_inc(logits_in, 1)

    @block.vector
    def _(dve):
        chain = Chain(dve, steps)
        nc.vector.tensor_reduce(colsum, m.xn[:, 0:NT - 1, :].rearrange("p t d -> p d t"), AX.X, ALU.add).then_inc(summed, 1)
        dve.wait_ge(mean_in, 1)
        chain.next(nc.vector.tensor_scalar(mu, ps_mean, 1.0 / N, None, ALU.mult))
        nc.vector.tensor_copy(muw, mu.unsqueeze(2).to_broadcast([P, 2, P])).then_inc(wide_in, 1)
        dve.wait_ge(logits_in, 1)
        chain.next(nc.vector.tensor_tensor(rw, ps_logit, br, ALU.add))
        for n, (ready, done) in enumerate(((e1, e1d), (e2, e2d))):
            chain.next(nc.vector.tensor_reduce(top, rw, AX.X, ALU.max))
            nc.vector.tensor_scalar(rw, rw, top, None, ALU.subtract).then_inc(ready, 1)
            dve.wait_ge(done, 1)
            chain.next(nc.vector.tensor_reduce(tot, ex, AX.X, ALU.add))
            chain.next(nc.vector.reciprocal(tot, tot))
            chain.next(nc.vector.tensor_scalar(rw, ex, tot, None, ALU.mult))
            if n == 0:
                chain.next(nc.vector.tensor_scalar(scl, rw, float(N), 1e-30, ALU.mult, ALU.max))
                chain.next(nc.vector.reciprocal(scl, scl))
                chain.next(nc.vector.tensor_scalar(scl, scl, capacity, 1.0, ALU.mult, ALU.min))
                chain.next(nc.vector.tensor_tensor(rw, rw, scl, ALU.mult))
        rank_of(nc, m, chain, rw.unsqueeze(1), gt, eq, rank.unsqueeze(1), NE, 1)
        for k in range(2):
            chain.next(nc.vector.tensor_scalar(sel, rank, float(k), None, ALU.is_equal))
            chain.next(nc.vector.tensor_tensor(ex, sel, rw, ALU.mult))
            chain.next(nc.vector.tensor_reduce(val[:, k:k + 1], ex, AX.X, ALU.add))
            chain.next(nc.vector.tensor_tensor(ex, sel, m.iota[:, 0:NE], ALU.mult))
            chain.next(nc.vector.tensor_reduce(num[:, k:k + 1], ex, AX.X, ALU.add))
        nc.vector.tensor_tensor(diff, val[:, 1:2], val[:, 0:1], ALU.subtract).then_inc(e3, 1)
        dve.wait_ge(e3d, 1)
        chain.next(nc.vector.tensor_scalar(tot, diff, 1.0, None, ALU.add))
        chain.next(nc.vector.reciprocal(tot, tot))
        chain.next(nc.vector.tensor_copy(m.gates[:, 0, :], tot.to_broadcast([P, NT])))
        chain.next(nc.vector.tensor_tensor(tot, tot, diff, ALU.mult))
        chain.next(nc.vector.tensor_copy(m.gates[:, 1, :], tot.to_broadcast([P, NT])))
        for k in range(2):
            for c in range(2):
                chain.next(nc.vector.tensor_scalar(offs[:, 7 * k + c:7 * k + c + 1], num[:, k:k + 1], float(D), float(c * P), ALU.mult, ALU.add))
            for c in range(4):
                chain.next(nc.vector.tensor_scalar(offs[:, 7 * k + 2 + c:7 * k + 3 + c], num[:, k:k + 1], float(F), float(c * P), ALU.mult, ALU.add))
            chain.next(nc.vector.tensor_tensor(offs[:, 7 * k:7 * k + 6], offs[:, 7 * k:7 * k + 6], m.pid[:, 0:1].to_broadcast([P, 6]), ALU.add))
            chain.next(nc.vector.tensor_copy(offs[:, 7 * k + 6:7 * k + 7], num[:, k:k + 1]))
        nc.vector.tensor_copy(offs_i[:, :], offs).then_inc(index, 1)

    @block.scalar
    def _(act):
        for ready, done in ((e1, e1d), (e2, e2d)):
            act.wait_ge(ready, 1)
            nc.scalar.activation(ex, rw, ACT.Exp).then_inc(done, 1)
        act.wait_ge(e3, 1)
        nc.scalar.activation(diff, diff, ACT.Exp).then_inc(e3d, 1)

    @block.gpsimd
    def _(pool):
        def gather(out, table, col):
            nc.gpsimd.indirect_dma_start(out=out, out_offset=None, in_=table,
                                         in_offset=bass.IndirectOffsetOnAxis(ap=offs_i[:, col:col + 1], axis=0)).then_inc(got, 16)

        pool.wait_ge(index, 1)
        for k in range(2):
            for c in range(2):
                gather(m.w1[k][:, c, :], w1_in.rearrange("e d f -> (e d) f"), 7 * k + c)
            for c in range(4):
                gather(m.w2[k][:, c, :], w2_in.rearrange("e f d -> (e f) d"), 7 * k + 2 + c)
                gather(m.b1[k][:, c:c + 1], b1_in.rearrange("e (f o) -> (e f) o", o=1), 7 * k + 2 + c)
            gather(m.b2[k][:, :], b2_in, 7 * k + 6)
        pool.wait_ge(got, 2 * 11 * 16)


def experts(nc, block, m, name, ne, out, params=None):
    loaded = [m.sem(f"{name}_loaded{s}") for s in range(2)]
    hidden, gelud, made, added = (m.sem(f"{name}_{s}") for s in ("hidden", "gelud", "made", "added"))
    half = GN * P // 2
    ps_h = [m.psum_all[:, 2 * b:2 * b + 2, 0:half] for b in range(2)]
    ps_y = [m.psum[4 + j % 4][:, 0:D] for j in range(GN)]
    trips = NT // GN
    KF = F // P
    ht = m.work[:, 0:KF * GN * P].rearrange("p (k n) -> p k n", k=KF)


    @block.sync
    def _(sp):
        if params is not None:
            w1_in, b1_in, w2_in, b2_in = params
            for e in range(ne):
                s = e % 2
                if e >= 2:
                    sp.wait_ge(made, NT * (e - 1) + 1)
                sp.dma_start(m.w1[s][:, :, :], w1_in[e].rearrange("(k p) f -> p k f", p=P)).then_inc(loaded[s], 16)
                sp.dma_start(m.w2[s][:, :, :], w2_in[e].rearrange("(k p) d -> p k d", p=P)).then_inc(loaded[s], 16)
                with nc.allow_non_contiguous_dma(reason="512 biases to the partitions of their features"):
                    sp.dma_start(m.b1[s][:, :], b1_in[e].rearrange("(k p) -> p k", p=P)).then_inc(loaded[s], 16)
                sp.dma_start(m.b2[s][0:1, :], b2_in[e:e + 1, :]).then_inc(loaded[s], 16)

    @block.tensor
    def _(pe):
        pe.sem_inc(made, 1)
        for e in range(ne):
            s = e % 2
            if params is not None:
                pe.wait_ge(loaded[s], 64 * (e // 2 + 1))
            w1, w2, b2 = m.w1[s], m.w2[s], m.b2[s]
            with pe.Fori(0, trips) as i:
                for f in range(KF):
                    pe.wait_ge(gelud, i * KF + (e * trips * KF + f + 1))
                    for k in range(2):
                        for hf in range(2):
                            ins = nc.tensor.matmul(ps_h[f % 2][:, hf, :], w1[:, k, f * P:(f + 1) * P],
                                                   m.xt[:, k, bass.ds(i * (GN * P) + hf * half, half)], start=k == 0, stop=k == 1)
                    ins.then_inc(hidden, 1)
                pe.wait_ge(gelud, i * KF + (e * trips * KF + KF + 2))
                pe.wait_ge(added, i * GN + (e * NT + 1))
                for j in range(GN):
                    if j >= 4:
                        pe.wait_ge(added, i * GN + (e * NT + j - 2))
                    for k in range(KF):
                        nc.tensor.matmul(ps_y[j], ht[:, k, j * P:(j + 1) * P], w2[:, k, :], start=k == 0, stop=False)
                    nc.tensor.matmul(ps_y[j], m.ones[0:1, :], b2[0:1, :], start=False, stop=True).then_inc(made, 1)

    @block.scalar
    def _(act):
        act.sem_inc(gelud, 2)
        for e in range(ne):
            if params is not None:
                act.wait_ge(loaded[e % 2], 64 * (e // 2 + 1))
            with act.Fori(0, trips) as i:
                for f in range(KF):
                    act.wait_ge(hidden, i * KF + (e * trips * KF + f + 1))
                    act.wait_ge(made, i * GN + (e * NT + 1))
                    nc.scalar.activation(ht[:, f, :].rearrange("p (a n) -> p a n", a=2), ps_h[f % 2], ACT.Gelu,
                                         bias=m.b1[e % 2][:, f:f + 1]).then_inc(gelud, 1)

    @block.vector
    def _(dve):
        dve.sem_inc(added, 1)
        for e in range(ne):
            with dve.Fori(0, trips) as i:
                for j in range(GN):
                    t = i * GN + j
                    dve.wait_ge(made, i * GN + (e * NT + j + 2))
                    if e:
                        dve.wait_ge(added, i * GN + (e * NT + j - NT + 2))
                    nc.vector.scalar_tensor_tensor(out[:, t, :], ps_y[j], m.gates[:, e, bass.ds(t, 1)], out[:, t, :],
                                                   ALU.mult, ALU.add).then_inc(added, 1)


def finish(nc, block, m, gamma_in, beta_in, y_out):
    loaded, steps, made, stored = m.sem("fin_loaded"), m.sem("fin_steps"), m.sem("fin_made"), m.sem("fin_stored")

    @block.sync
    def _(sp):
        sp.dma_start(m.bias[:, :], gamma_in.partition_broadcast(P)).then_inc(loaded, 16)
        sp.dma_start(m.prod[:, 0, :], beta_in.partition_broadcast(P)).then_inc(loaded, 16)
        sp.wait_ge(made, 1)
        sp.dma_start(y_out[0:(NT - 1) * P, :].rearrange("(t p) d -> p t d", p=P), m.xn[:, 0:NT - 1, :]).then_inc(stored, 16)
        sp.dma_start(y_out[(NT - 1) * P:N, :], m.xn[0:LAST, NT - 1, :]).then_inc(stored, 16)
        sp.wait_ge(stored, 32)

    @block.vector
    def _(dve):
        chain = Chain(dve, steps)
        dve.wait_ge(loaded, 32)
        chain.next(nc.vector.tensor_tensor(m.x[:, :, :], m.x[:, :, :], m.prod[:, 0, :].unsqueeze(1).to_broadcast([P, NT, D]), ALU.add))
        chain.next(nc.vector.tensor_tensor(m.xn[:, :, :], m.xn[:, :, :], m.bias[:, :].unsqueeze(1).to_broadcast([P, NT, D]), ALU.mult))
        nc.vector.tensor_tensor(m.xn[:, :, :], m.xn[:, :, :], m.x[:, :, :], ALU.add).then_inc(made, 1)



class Memory:

    turn = 0
    semaphores = None


def memory(nc, ctx):
    m = Memory()

    def sb(name, shape, dt=F32):
        return ctx.enter_context(nc.sbuf_tensor(name, shape, dt))

    m.dma_sem = lambda name: ctx.enter_context(nc.semaphore(name))
    m.x = sb("x", [P, NT, D])
    m.xn = sb("xn", [P, NT, D])
    m.xt = sb("xt", [P, 2, NT * P])
    m.hidden = m.xt[:, :, :].rearrange("p k n -> p (k n)").rearrange("p (t d) -> p t d", t=NT)
    m.acc = sb("acc", [P, NT + 1, D + 4 * HEADS])
    m.den = sb("den", [P, NT, HEADS])
    m.work = sb("work", [P, WORK])
    m.rec = [sb(f"rec{k}", [P, n * ET * 3]) for k, n in enumerate((NCH, NCHG, NCH))]
    m.bucket = [sb(f"bucket{k}", [P, n], I32) for k, n in enumerate((NCH, NCHG, NCH))]
    flat = m.xt[:, :, :].rearrange("p k n -> p (k n)")
    cols = [flat[:, 400 * k:400 * (k + 1)] for k in range(7)]
    m.sort_key, m.sort_val, m.sort_lo, m.sort_place = (c.bitcast(I32) for c in cols[0:4])
    m.sort_hi, m.sort_w, m.sort_hi2 = cols[4:7]
    m.sort_small = flat[:, 2800:2800 + 8 * 32].rearrange("p (k n) -> p k n", k=8)
    m.sort_small_i = flat[:, 3100:3100 + NT].bitcast(I32)
    late = sb("records2", [P, 4 * columns_for(E)])
    spaces = (flat[:, 3200:4800], flat[:, 4800:4800 + 4 * columns_for(EG)], late[:, :])
    m.record = [b[:, 0:3 * b.shape[1] // 4].rearrange("p (f k) -> p f k", k=3) for b in spaces]
    m.row = [b[:, 3 * b.shape[1] // 4:].bitcast(I32) for b in spaces]
    m.trips = sb("trips", [P, 3], I32)
    m.stage_rec = [sb(f"stage_rec{s}", [P, COPIES // 2, 3]) for s in range(2)]
    m.stage_row = [sb(f"stage_row{s}", [P, COPIES // 2], I32) for s in range(2)]
    m.ident, m.before, m.ones, m.iota = (sb(n, [P, P]) for n in ("ident", "before", "ones", "iota"))
    m.iota_i = m.work[:, 0:P].bitcast(I32)
    m.iota_c = m.work[:, P:P + NCH].bitcast(I32)
    m.pid_i = m.work[:, 300:302].bitcast(I32)
    m.iotac, m.pid, m.dummy, m.lower = sb("iotac", [P, NCH]), sb("pid", [P, 2]), sb("dummy_rows", [P, 2]), sb("lower", [P, 8, 8])
    m.stats = sb("stats", [P, 3, NT])
    m.bias, m.prod, m.att = sb("bias", [P, D]), sb("prod", [P, 2, D]), sb("att", [P, 2, D])
    m.small, m.idle = sb("small", [P, 16]), sb("idle", [P, 1])
    m.gates = sb("gates", [P, 4, NT])
    m.expert_rows = sb("expert_rows", [P, 14], I32)

    m.slot_x = [m.work[:, 256 * j:256 * (j + 1)] for j in range(GN)]
    m.slot_xt = [m.work[:, 1280 + 256 * j:1280 + 256 * (j + 1)].rearrange("p (k n) -> p k n", k=2) for j in range(GN)]
    m.w_mat = m.work[:, 2560:3072].rearrange("p (k n) -> p k n", k=2)
    at = [0]

    def view(*shape):
        n = 1
        for d in shape:
            n *= d
        v = m.work[:, at[0]:at[0] + n]
        at[0] += n
        if len(shape) == 2:
            v = v.rearrange("p (a b) -> p a b", a=shape[0])
        return v

    RW = D + 2 * HEADS
    m.rows = [view(ET, RW) for _ in range(4)]
    m.hot = [view(ET, P) for _ in range(4)]
    m.pen = view(ET, P)
    m.offer = [view(ET, HEADS * P) for _ in range(2)]
    m.hott = [view(ET, P) for _ in range(4)]
    m.best = view(HEADS * P)
    m.msg = [view(ET * (D + HEADS)) for _ in range(2)]
    m.stage = [view(ET, 3) for _ in range(4)]
    m.stage_idx = [view(ET).bitcast(I32) for _ in range(4)]
    m.adm = [view(3 * HEADS) for _ in range(2)]
    m.old = view(3 * HEADS)
    m.drop = [view(HEADS) for _ in range(2)]
    m.fac = [view(HEADS) for _ in range(2)]
    m.score = [view(ET * HEADS) for _ in range(2)]
    m.wexp = [view(ET * HEADS) for _ in range(2)]
    assert at[0] <= WORK, at[0]
    at[0] = 4 * GN * P
    m.w1 = [view(2, F) for _ in range(2)]
    m.w2 = [view(4, D) for _ in range(2)]
    m.b1 = [view(4) for _ in range(2)]
    m.b2 = [view(D) for _ in range(2)]
    assert at[0] <= 12000

    m.psum_all = ctx.enter_context(nc.psum_tensor("psum", [P, 8, 512], F32))
    m.psum = [m.psum_all[:, k, :] for k in range(8)]
    return m


SEMAPHORES = 40


class Stage:

    def __init__(self, nc, m):
        self.nc, self.m = nc, m
        if m.semaphores is None:
            m.semaphores = max(nc.free_semaphores) + 1 - 2 * SEMAPHORES

    def __enter__(self):
        nc, m = self.nc, self.m
        self.ctx = ExitStack()
        mine, other = m.semaphores + m.turn * SEMAPHORES, m.semaphores + (1 - m.turn) * SEMAPHORES
        numbers = iter(range(mine, mine + SEMAPHORES))
        m.sem = lambda name: self.ctx.enter_context(nc.semaphore(name, num=next(numbers)))
        self.block = nc.Block()
        block = self.block.__enter__()

        @block.sync
        def _(sp):
            sp.sem_clear(range(other, other + SEMAPHORES))

        m.turn = 1 - m.turn
        return block

    def __exit__(self, *error):
        self.block.__exit__(*error)
        return self.ctx.__exit__(*error)


def program(nc, a, y_out):
    with ExitStack() as ctx:
        m = memory(nc, ctx)
        table_sum = nc.dram_tensor("table_sum", [NT * P, D], F32).ap()
        table_gate = nc.dram_tensor("table_gate", [NT * P, 24], F32).ap()
        table_att = nc.dram_tensor("table_att", [NT * P, D + 2 * HEADS], F32).ap()
        sorted_dram = [[nc.dram_tensor(f"sorted{k}_{c}", [P * ET * n + P, 3], F32).ap() for c in range(COPIES)]
                       for k, n in enumerate((NCH, NCHG, NCH))]
        xn, hidden = m.xn[:, :, :], m.hidden

        with Stage(nc, m) as block:
            setup(nc, block, m, a["x"])
        graphs = ((a["src"], a["dst"], a["edge_weight"], NCH),
                  (a["L0_ffn_edge_index"][1], a["L0_ffn_edge_index"][0], None, NCHG),
                  (a["dst"], a["src"], None, NCH))

        def place(block, k):
            key, val, w, nch = graphs[k]
            place_edges(nc, block, m, f"place{k}", key, val, w, nch, sorted_dram[k], m.record[k], m.row[k], m.bucket[k][:, :], m.trips[:, k:k + 1])

        def scatter(block, k):
            scatter_edges(nc, block, m, f"scatter{k}", graphs[k][0].shape[0], sorted_dram[k], m.record[k], m.row[k])

        def merge(block, k):
            merge_edges(nc, block, m, f"merge{k}", graphs[k][3], sorted_dram[k], m.rec[k][:, :])

        with Stage(nc, m) as block:
            place(block, 0)
        with Stage(nc, m) as block:
            scatter(block, 0)
            normed = m.sem("norm0_done")
            norm_rows(nc, block, m, "norm0", m.x[:, :, :], xn, done=normed)
            project(nc, block, m, "sup", a["L0_gnn_weight"], D, m.xn, table_sum, after=normed)
            place(block, 1)
            place(block, 2)
        with Stage(nc, m) as block:
            scatter(block, 1)
            merge(block, 0)
        with Stage(nc, m) as block:
            sum_edges(nc, block, m, "sum", table_sum, m.rec[0], m.bucket[0], m.trips[0:1, 0:1], NCH)
        with Stage(nc, m) as block:
            add_sums(nc, block, m, "addsum", a["L0_gnn_bias"])
            norm_rows(nc, block, m, "norm1", m.x[:, :, :], xn, square=hidden)
            merge(block, 1)

        with Stage(nc, m) as block:
            project(nc, block, m, "gate", a["L0_ffn_W_gat"], 16, m.xn, table_gate, a["L0_ffn_att_src"], a["L0_ffn_att_dst"], keep_t=m.xt)
        with Stage(nc, m) as block:
            attend_edges(nc, block, m, "gatt", 16, table_gate, m.rec[1], m.bucket[1], m.trips[0:1, 1:2], NCHG)
        with Stage(nc, m) as block:
            gate_nodes(nc, block, m, "gates", a["L0_ffn_b_gat"], a["L0_ffn_ln_gamma"], a["L0_ffn_ln_beta"])
        with Stage(nc, m) as block:
            experts(nc, block, m, "ffn0", 4, m.x, (a["L0_ffn_W1"], a["L0_ffn_b1"], a["L0_ffn_W2"], a["L0_ffn_b2"]))
            scatter(block, 2)

        with Stage(nc, m) as block:
            norm_rows(nc, block, m, "norm2", m.x[:, :, :], xn, square=hidden)
            merge(block, 2)
        layers = (("W1", "as1", "ad1", "b1"), ("W2", "as2", "ad2", "b2"), ("WN", "asN", "adN", "bN"))
        for k, (w, att_src, att_dst, b) in enumerate(layers):
            with Stage(nc, m) as block:
                project(nc, block, m, f"l{k}p", a["L1_gnn_" + w], D, m.xn if k == 0 else hidden, table_att,
                        a["L1_gnn_" + att_src], a["L1_gnn_" + att_dst])
            with Stage(nc, m) as block:
                attend_edges(nc, block, m, f"l{k}e", D, table_att, m.rec[2], m.bucket[2], m.trips[0:1, 2:3], NCH)
            with Stage(nc, m) as block:
                finish_layer(nc, block, m, f"l{k}f", k, a["L1_gnn_" + b])

        with Stage(nc, m) as block:
            norm_rows(nc, block, m, "norm3", m.x[:, :, :], xn)
        with Stage(nc, m) as block:
            turn_rows(nc, block, m, "turn")
            route(nc, block, m, "route", a["L1_ffn_Wr"], a["L1_ffn_br"], a["L1_ffn_W1"], a["L1_ffn_b1"], a["L1_ffn_W2"], a["L1_ffn_b2"])
        with Stage(nc, m) as block:
            experts(nc, block, m, "ffn1", 2, m.xn)
        with Stage(nc, m) as block:
            norm_rows(nc, block, m, "norm4", xn, xn)
        with Stage(nc, m) as block:
            finish(nc, block, m, a["L1_ffn_gamma"], a["L1_ffn_beta"], y_out)


_INS = ["x", "src", "dst", "edge_weight", "L0_gnn_weight", "L0_gnn_bias", "L0_ffn_W_gat", "L0_ffn_att_src", "L0_ffn_att_dst",
        "L0_ffn_b_gat", "L0_ffn_ln_gamma", "L0_ffn_ln_beta", "L0_ffn_W1", "L0_ffn_b1", "L0_ffn_W2", "L0_ffn_b2",
        "L0_ffn_edge_index", "L1_gnn_W1", "L1_gnn_as1", "L1_gnn_ad1", "L1_gnn_b1", "L1_gnn_W2", "L1_gnn_as2", "L1_gnn_ad2",
        "L1_gnn_b2", "L1_gnn_WN", "L1_gnn_asN", "L1_gnn_adN", "L1_gnn_bN", "L1_ffn_Wr", "L1_ffn_br", "L1_ffn_W1", "L1_ffn_b1",
        "L1_ffn_W2", "L1_ffn_b2", "L1_ffn_gamma", "L1_ffn_beta"]


def kernel(**inputs):
    import numpy as _np
    import concourse.bacc as _bacc
    from concourse import mybir as _mybir
    from concourse.bass_utils import run_bass_kernel_spmd as _run

    nc = _bacc.Bacc("TRN2", target_bir_lowering=False, num_devices=1)
    arrays, args = {}, {}
    for name in _INS:
        arr = _np.ascontiguousarray(inputs[name])
        arrays[f"in_{name}_dram"] = arr
        args[name] = nc.dram_tensor(f"in_{name}_dram", arr.shape, _mybir.dt.from_np(arr.dtype), kind="ExternalInput").ap()
    y = nc.dram_tensor("out_0_dram", (N, D), F32, kind="ExternalOutput").ap()
    program(nc, args, y)
    r = _run(nc, [arrays], core_ids=[0])
    return r.results[0]["out_0_dram"]
```
